# Optimizing a Trainium2 kernel written in Bass

```python
import numpy as np
import jax
import jax.numpy as jnp

def _softmax(x, axis=-1):
    return jax.nn.softmax(x, axis=axis)

def _gelu(x):
    return jax.nn.gelu(x, approximate=True)

def _silu(x):
    return jax.nn.silu(x)

def _sigmoid(x):
    return jax.nn.sigmoid(x)

def _layernorm(x, axis=-1, eps=1e-05):
    m = jnp.mean(x, axis=axis, keepdims=True)
    v = jnp.var(x, axis=axis, keepdims=True)
    return (x - m) / jnp.sqrt(v + eps)

def _scatter_add(tgt, idx, src, axis=0):
    return tgt.at[idx].add(src)

def _segment_sum(src, seg, n):
    return jax.ops.segment_sum(src, seg, n)
kernel_name = 'mk_cond_resid_d1_seqx_r2_4bcdfd'

def setup_inputs(seed: int=0):
    np.random.seed(seed)
    _w = jnp.asarray

    def _rec_inputs():
        import jax
        import jax.numpy as jnp
        _rk = jax.random.key(seed)
        x = 4.136e-05 + 0.9999 * jax.random.normal(jax.random.fold_in(_rk, 1), (32, 512, 512), jnp.float32)
        _lenS = 512 - jax.random.randint(jax.random.fold_in(_rk, 7), (32,), 0, max(1, 512 // 4) + 1, jnp.int32)
        _lenS2 = 512 - jax.random.randint(jax.random.fold_in(_rk, 8), (32,), 0, max(1, 512 // 4) + 1, jnp.int32)
        cond_1024 = -0.00608245 + 1.00131 * jax.random.normal(jax.random.fold_in(_rk, 11), (32, 512), jnp.float32)
        return (x, cond_1024)
    x, cond_1024 = _rec_inputs()

    def _L0_cond_setup():
        import jax, jax.numpy as jnp
        import numpy as np
        B, T, D_IN, V_IN, E = (64, 128, 512, 512, 512)
        key = jax.random.key(seed)
        ks = jax.random.split(key, 16)
        s = 0.01
        return {'video': jax.random.normal(ks[0], (B, V_IN), jnp.float32), 'seq': jax.random.normal(ks[1], (B, T, D_IN), jnp.float32), 'W_z': jax.random.normal(ks[2], (D_IN, E), jnp.float32) * s, 'U_z': jax.random.normal(ks[3], (E, E), jnp.float32) * s, 'C_z': jax.random.normal(ks[4], (V_IN, E), jnp.float32) * s, 'b_z': jnp.zeros((E,), jnp.float32), 'W_r': jax.random.normal(ks[5], (D_IN, E), jnp.float32) * s, 'U_r': jax.random.normal(ks[6], (E, E), jnp.float32) * s, 'C_r': jax.random.normal(ks[7], (V_IN, E), jnp.float32) * s, 'b_r': jnp.zeros((E,), jnp.float32), 'W': jax.random.normal(ks[8], (D_IN, E), jnp.float32) * s, 'U': jax.random.normal(ks[9], (E, E), jnp.float32) * s, 'C': jax.random.normal(ks[10], (V_IN, E), jnp.float32) * s, 'b': jnp.zeros((E,), jnp.float32)}
    _L0_cond_all = _L0_cond_setup()
    _L0_cond_in = {k: v for k, v in _L0_cond_all.items() if k in ('W_z', 'U_z', 'C_z', 'b_z', 'W_r', 'U_r', 'C_r', 'b_r', 'W', 'U', 'C', 'b')}
    del _L0_cond_all
    return {'x': x, 'cond_1024': cond_1024, 'L0_cond_W_z': _L0_cond_in['W_z'], 'L0_cond_U_z': _L0_cond_in['U_z'], 'L0_cond_C_z': _L0_cond_in['C_z'], 'L0_cond_b_z': _L0_cond_in['b_z'], 'L0_cond_W_r': _L0_cond_in['W_r'], 'L0_cond_U_r': _L0_cond_in['U_r'], 'L0_cond_C_r': _L0_cond_in['C_r'], 'L0_cond_b_r': _L0_cond_in['b_r'], 'L0_cond_W': _L0_cond_in['W'], 'L0_cond_U': _L0_cond_in['U'], 'L0_cond_C': _L0_cond_in['C'], 'L0_cond_b': _L0_cond_in['b']}

def reference(x, cond_1024, L0_cond_W_z, L0_cond_U_z, L0_cond_C_z, L0_cond_b_z, L0_cond_W_r, L0_cond_U_r, L0_cond_C_r, L0_cond_b_r, L0_cond_W, L0_cond_U, L0_cond_C, L0_cond_b):
    import jax
    import jax.numpy as jnp

    def _L0_cond_ref(video, seq, W_z, U_z, C_z, b_z, W_r, U_r, C_r, b_r, W, U, C, b):
        import jax, jax.numpy as jnp
        import numpy as np
        B, T, D_IN, V_IN, E = (64, 128, 512, 512, 512)
        vz = video @ C_z + b_z
        vr = video @ C_r + b_r
        vh = video @ C + b
        xz = jnp.einsum('btd,de->bte', seq, W_z)
        xr = jnp.einsum('btd,de->bte', seq, W_r)
        xh = jnp.einsum('btd,de->bte', seq, W)

        def step(h, xs):
            xzt, xrt, xht = xs
            z = jax.nn.sigmoid(xzt + h @ U_z + vz)
            r = jax.nn.sigmoid(xrt + h @ U_r + vr)
            hh = jnp.tanh(xht + r * h @ U + vh)
            h_new = (1.0 - z) * h + z * hh
            return (h_new, h_new)
        h0 = jnp.zeros((seq.shape[0], U.shape[0]), seq.dtype)
        xs = (jnp.swapaxes(xz, 0, 1), jnp.swapaxes(xr, 0, 1), jnp.swapaxes(xh, 0, 1))
        _, out_t = jax.lax.scan(step, h0, xs)
        return jnp.swapaxes(out_t, 0, 1)
    x = x + _L0_cond_ref(cond_1024, x, L0_cond_W_z, L0_cond_U_z, L0_cond_C_z, L0_cond_b_z, L0_cond_W_r, L0_cond_U_r, L0_cond_C_r, L0_cond_b_r, L0_cond_W, L0_cond_U, L0_cond_C, L0_cond_b)
    return x

_drawn_inputs = setup_inputs


def setup_inputs(seed=0):
    import zlib

    import numpy as np

    out = dict(_drawn_inputs(seed))
    spreads = {'L0_cond_b_z': (0.0, 0.8), 'L0_cond_b_r': (0.0, 0.8), 'L0_cond_b': (0.0, 0.1)}
    factors = {'L0_cond_W_z': 3.823,
     'L0_cond_U_z': 8.0,
     'L0_cond_C_z': 4.656,
     'L0_cond_W_r': 8.0,
     'L0_cond_U_r': 8.0,
     'L0_cond_C_r': 8.0}
    for name, (base, spread) in spreads.items():
        noise = np.random.default_rng([zlib.crc32(name.encode()), seed]).standard_normal(out[name].shape)
        drawn = base * np.exp(spread * noise) if base else spread * noise
        out[name] = jnp.asarray(drawn.astype(out[name].dtype))
    for name, factor in factors.items():
        out[name] = (out[name] * factor).astype(out[name].dtype)
    return out
```

```python
import concourse.bass as bass
from concourse import mybir
from contextlib import ExitStack


def conditioned_gru_residual_kernel(nc, x, cond, W_z, U_z, C_z, b_z, W_r, U_r, C_r, b_r, W_h, U_h, C_h, b_h, out):
    f32, f16, i32 = mybir.dt.float32, mybir.dt.float16, mybir.dt.int32
    ALU, ACT, AX = mybir.AluOpType, mybir.ActivationFunctionType, mybir.AxisListType

    B, T, D = x.shape
    E = U_z.shape[1]
    P = 128
    KD = D // P
    M = E // P
    G = 3
    R, Z, C = 0, 1, 2
    TU = P // B
    NU = 2
    TB = TU * NU
    COLS = TB * B
    BODY = 2
    BLOCKS = T // TB
    PASSES = BLOCKS // BODY
    GROUPS = G * M
    HM = M // 2
    HSCALE = 2048.0
    UPOW = 14
    assert KD == M and P % B == 0 and BLOCKS % BODY == 0

    x_rows = x.rearrange("b (n u t) d -> n t b u d", u=NU, t=TU)
    out_rows = out.rearrange("b (n u t) d -> n t b u d", u=NU, t=TU)

    ctx = ExitStack()
    with ctx:
        def sb(name, shape, dt):
            return ctx.enter_context(nc.sbuf_tensor(name, shape, dt))

        def bank(name):
            return ctx.enter_context(nc.psum_tensor(name, [P, 512], f32))

        def sem(name):
            return ctx.enter_context(nc.semaphore(name))

        def pair(name):
            return [sem(f"{name}{j}") for j in range(2)]

        u_stage = sb("u_stage", [P, G, KD, E], f32)
        c_stage = sb("c_stage", [P, G, KD, E], f32)
        u_hi = sb("u_hi", [P, G, KD, E], f16)
        u_lo = sb("u_lo", [P, G, KD, E], f16)
        w_in = sb("w_in", [P, G, KD, E], f32)
        x_nat = [sb(f"x_nat{j}", [P, NU, D], f32) for j in range(BODY)]
        x_t = [sb(f"x_t{j}", [P, KD, NU, P], f32) for j in range(BODY)]
        proj = [sb(f"proj{j}", [P, GROUPS, TB, B], f32) for j in range(BODY)]
        result = [sb(f"result{j}", [P, NU, E], f32) for j in range(BODY)]
        state = sb("state", [P, M, TB, B], f32)
        state_parts = sb("state_parts", [P, M, 2 * B], f16)
        reset_parts = sb("reset_parts", [P, M, 2 * B], f16)
        reset_full = sb("reset_full", [P, M, B], f32)
        pre_a = sb("pre_a", [P, G, M, B], f32)
        pre_b = sb("pre_b", [P, G, M, B], f32)
        gate = sb("gate", [P, G, M, B], f32)
        keep = sb("keep", [P, M, B], f32)
        kept = sb("kept", [P, M, B], f32)
        taken = sb("taken", [P, M, B], f32)
        ident = sb("ident", [P, P], f32)
        cond_nat = sb("cond_nat", [B, D], f32)
        cond_t = sb("cond_t", [P, KD, B], f32)
        bias_nat = sb("bias_nat", [GROUPS, P], f32)
        bias_t = sb("bias_t", [P, GROUPS], f32)
        base = sb("base", [P, GROUPS, B], f32)
        u_max = sb("u_max", [P, G], f32)
        top = sb("top", [G, 1], f32)
        power = sb("power", [G, 1], f32)
        power_diag = sb("power_diag", [G, G], f32)
        ones = sb("ones", [G, P], f32)
        powers = sb("powers", [P, G], f32)
        up = sb("up", [P, G], f32)
        down = sb("down", [P, G], f32)

        r_bank, c_bank = [bank("r_bank0"), bank("r_bank1")], [bank("c_bank0"), bank("c_bank1")]
        z_bank = bank("z_bank")
        p_bank = [bank("p_bank0"), bank("p_bank1")]
        t_bank = bank("t_bank")

        def sums(b, blocks):
            return b[:, 0:blocks * 2 * B].rearrange("p (m c) -> p m c", m=blocks)

        s_const, s_const1 = sem("s_const"), sem("s_const1")
        s_u_in, s_c_in, s_w_in, s_small_in = sem("s_u_in"), sem("s_c_in"), sem("s_w_in"), sem("s_small_in")
        s_cond_mm, s_cond_t = sem("s_cond_mm"), sem("s_cond_t")
        s_base_mm, s_base = sem("s_base_mm"), sem("s_base")
        s_max, s_max_mm, s_pow, s_pow_mm = sem("s_max"), sem("s_max_mm"), sem("s_pow"), sem("s_pow_mm")
        s_link, s_split = sem("s_link"), sem("s_split")
        x_in, result_in, result_out = pair("x_in"), pair("result_in"), pair("result_out")
        x_turned, x_t_ready = sem("x_turned"), sem("x_t_ready")
        proj_mm, proj_ready = sem("proj_mm"), sem("proj_ready")
        out_turned, out_ready = sem("out_turned"), sem("out_ready")
        r_mm, z_mm, c_mm = pair("r_mm"), sem("z_mm"), pair("c_mm")
        r_part, r_pre, r_gate = pair("r_part"), pair("r_pre"), pair("r_gate")
        rh_hi, rh_full, rh_lo = pair("rh_hi"), pair("rh_full"), pair("rh_lo")
        z_part, z_pre, z_gate, z_keep, z_kept = (sem(n) for n in ("z_part", "z_pre", "z_gate", "z_keep", "z_kept"))
        c_part, c_pre, c_gate = pair("c_part"), pair("c_pre"), pair("c_gate")
        h_take, h_hi, h_full, h_lo = pair("h_take"), pair("h_hi"), pair("h_full"), pair("h_lo")

        block = ctx.enter_context(nc.Block())

        def halves(j):
            return slice(j * HM, (j + 1) * HM)

        @block.sync
        def _(sp):
            for g, (w, c, u) in enumerate(((W_r, C_r, U_r), (W_z, C_z, U_z), (W_h, C_h, U_h))):
                sp.dma_start(u_stage[:, g], u.rearrange("(k p) e -> p k e", p=P)).then_inc(s_u_in, 16)
                sp.dma_start(c_stage[:, g], c.rearrange("(k p) e -> p k e", p=P)).then_inc(s_c_in, 16)
                sp.dma_start(w_in[:, g], w.rearrange("(k p) e -> p k e", p=P)).then_inc(s_w_in, 16)

            def load_x(n, j, buffers, done):
                for t in range(TU):
                    sp.dma_start(buffers[j][t * B:(t + 1) * B], x_rows[n, t]).then_inc(done[j], 16)

            for j in range(BODY):
                load_x(j, j, result, result_in)

            def block_of_steps(i, j, last):
                n = i * BODY + j
                tiles = NU * n + NU + 1 if last else sp.snap(NU * n + NU + 1)
                if not last:
                    sp.wait_ge(x_t_ready, NU * n + NU)
                    load_x(n + BODY, j, x_nat, x_in)
                sp.wait_ge(out_ready, tiles)
                for t in range(TU):
                    sp.dma_start(out_rows[n, t], result[j][t * B:(t + 1) * B]).then_inc(result_out[j], 16)
                sp.wait_ge(result_out[j], (i + 1) * 16 * TU)
                if not last:
                    load_x(n + BODY, j, result, result_in)

            with sp.Fori(0, PASSES - 1) as i:
                for j in range(BODY):
                    block_of_steps(i, j, False)
            for j in range(BODY):
                block_of_steps(PASSES - 1, j, True)

        @block.gpsimd
        def _(pool):
            nc.gpsimd.memset(ident[:], 0.0).then_inc(s_const, 1)
            nc.gpsimd.memset(ones[:], 1.0).then_inc(s_const1, 1)
            nc.gpsimd.memset(state[:], 0.0).then_inc(s_const1, 1)
            nc.gpsimd.memset(state_parts[:], 0.0).then_inc(s_const1, 1)
            pool.wait_ge(s_const1, 3)
            for j in range(2):
                pool.sem_inc(h_hi[j], 1)
                pool.sem_inc(h_lo[j], 1)
            pool.wait_ge(s_const, 1)
            nc.gpsimd.affine_select(out=ident[:], in_=ident[:], compare_op=ALU.not_equal, fill=1.0, base=0,
                                    pattern=[[-1, P]], channel_multiplier=1).then_inc(s_const1, 1)

        @block.tensor
        def _(pe):
            pe.wait_ge(s_const1, 4)
            pe.wait_ge(s_small_in, 16 * (1 + G))
            for k in range(KD):
                nc.tensor.transpose(t_bank[:, k * B:(k + 1) * B], cond_nat[:, k * P:(k + 1) * P], ident[0:B, 0:B])
            nc.tensor.transpose(t_bank[:, KD * B:KD * B + GROUPS], bias_nat[:], ident[0:GROUPS, 0:GROUPS])\
                .then_inc(s_cond_mm, 1)
            pe.wait_ge(s_cond_t, 2)
            pe.wait_ge(s_c_in, 16 * G)
            for q in range(GROUPS):
                g, m = divmod(q, M)
                for k in range(KD):
                    last = nc.tensor.matmul(z_bank[:, q * B:(q + 1) * B], c_stage[:, g, k, m * P:(m + 1) * P],
                                            cond_t[:, k, :], start=(k == 0), stop=(k == KD - 1))
            last.then_inc(s_base_mm, 1)
            pe.wait_ge(s_max, 1)
            nc.tensor.transpose(r_bank[0][0:G, 0:P], u_max[:], ident[:]).then_inc(s_max_mm, 1)
            pe.wait_ge(s_pow, 1)
            nc.tensor.matmul(r_bank[1][:, 0:G], ones[:], power_diag[:], start=True, stop=True).then_inc(s_pow_mm, 1)

            def turn_x(n, j, u, loads):
                if u == 0:
                    pe.wait_ge(x_in[j], loads * 16 * TU)
                if not (isinstance(n, int) and n == 0 and u == 0):
                    pe.wait_ge(x_t_ready, n * NU + u)
                pe.wait_ge(out_ready, loads_out[0] + 1)
                for k in range(KD):
                    last = nc.tensor.transpose(t_bank[:, k * P:(k + 1) * P], x_nat[j][:, u, k * P:(k + 1) * P], ident[:])
                last.then_inc(x_turned, 1)

            loads_out = [0]

            def turn_state(n, u, turned):
                pe.wait_ge(x_t_ready, turned)
                pe.wait_ge(out_ready, NU * n + u + 1)
                for m in range(M):
                    last = nc.tensor.transpose(t_bank[:, m * P:(m + 1) * P], state[:, m, u * TU:(u + 1) * TU, :], ident[:])
                last.then_inc(out_turned, 1)

            def project(first, j, k0, k1):
                for f in range(k0, k1):
                    q, k = divmod(f, KD)
                    g, m = divmod(q, M)
                    if k == 0 and not (q < 2 and isinstance(first, int) and first == 0):
                        pe.wait_ge(proj_ready, first + (q - 1))
                    last = nc.tensor.matmul(p_bank[q % 2][:, 0:COLS], w_in[:, g, k, m * P:(m + 1) * P],
                                            x_t[j][:, k, :, :], start=(k == 0), stop=(k == KD - 1))
                    if k == KD - 1:
                        last.then_inc(proj_mm, 1)

            def times_u(g, banks, parts, hi_ready, lo_ready, done):
                per = M // len(banks)
                for half in range(2):
                    pe.wait_ge(hi_ready[0][half], hi_ready[1])
                    pe.wait_ge(lo_ready[0][half], lo_ready[1])
                    for m in range(M):
                        into = sums(banks[m // per], per)[:, m % per, :]
                        for k in range(half * HM, (half + 1) * HM):
                            first = half == 0 and k == 0 and m % per == 0
                            nc.tensor.matmul(into, u_hi[:, g, k, m * P:(m + 1) * P], parts[:, k, :],
                                             start=first, stop=False, skip_group_check=True)
                            last = nc.tensor.matmul(into[:, 0:B], u_lo[:, g, k, m * P:(m + 1) * P], parts[:, k, 0:B],
                                                    start=False, stop=(half == 1 and k == KD - 1),
                                                    skip_group_check=True)
                        if half == 1 and m % per == per - 1:
                            last.then_inc(done[m // per], 1)

            pe.wait_ge(s_cond_t, 2)
            for n in range(BODY):
                for u in range(NU):
                    turn_x(n, n, u, 1)
            pe.wait_ge(s_w_in, 16 * G)
            pe.wait_ge(x_t_ready, NU)
            project(0, 0, 0, GROUPS * KD)
            pe.wait_ge(s_split, 2 * G)

            FILL = GROUPS * KD // TB

            def block_of_steps(i, j, last):
                n = i * BODY + j
                fill = not (last and j == BODY - 1)
                turn = not last
                first = pe.snap(n * GROUPS + GROUPS) if not last else n * GROUPS + GROUPS
                for t in range(TB):
                    step = n * TB + t
                    now = pe.snap(step + 1) if not last else step + 1
                    times_u(R, r_bank, state_parts, (h_hi, now), (h_lo, now), r_mm)
                    times_u(Z, [z_bank], state_parts, (h_hi, now), (h_lo, now), [z_mm])
                    if t == 4:
                        loads_out[0] = n * NU + 0
                        turn_state(n, 0, n * NU + NU * BODY if turn else BLOCKS * NU)
                    if turn and t in (2, 3):
                        loads_out[0] = n * NU
                        turn_x(n + BODY, j, t - 2, i + 2)
                    if fill:
                        if t == 0:
                            pe.wait_ge(x_t_ready, NU * n + 2 * NU)
                        project(first, 1 - j, t * FILL, t * FILL + FILL // 2)
                    times_u(C, c_bank, reset_parts, (rh_hi, now), (rh_lo, now), c_mm)
                    if fill:
                        project(first, 1 - j, t * FILL + FILL // 2, (t + 1) * FILL)
                for half in range(2):
                    pe.wait_ge(h_full[half], now)
                turn_state(n, 1, n * NU + NU * BODY if turn else BLOCKS * NU)

            with pe.Fori(0, PASSES - 1) as i:
                for j in range(BODY):
                    block_of_steps(i, j, False)
            for j in range(BODY):
                block_of_steps(PASSES - 1, j, True)

        @block.scalar
        def _(act):
            act.dma_start(cond_nat[:], cond).then_inc(s_small_in, 16)
            for g, b in enumerate((b_r, b_z, b_h)):
                act.dma_start(bias_nat[g * M:(g + 1) * M], b.rearrange("(m p) -> m p", p=P)).then_inc(s_small_in, 16)
            for j in range(BODY):
                for t in range(TU):
                    act.dma_start(x_nat[j][t * B:(t + 1) * B], x_rows[j, t]).then_inc(x_in[j], 16)

            def copy_x(n, j, u):
                act.wait_ge(x_turned, NU * n + u + 1)
                nc.scalar.activation(x_t[j][:, :, u, :], t_bank[:, 0:KD * P].rearrange("p (k c) -> p k c", k=KD),
                                     ACT.Copy).then_inc(x_t_ready, 1)

            for n in range(BODY):
                for u in range(NU):
                    copy_x(n, n, u)

            def block_of_steps(i, j, last):
                n = i * BODY + j
                for t in range(TB):
                    now = n * TB + t + 1 if last else act.snap(n * TB + t + 1)
                    for half in range(2):
                        act.wait_ge(r_pre[half], now)
                        nc.scalar.activation(gate[:, R, halves(half)], pre_b[:, R, halves(half)], ACT.Sigmoid)\
                            .then_inc(r_gate[half], 1)
                    act.wait_ge(z_pre, now)
                    nc.scalar.activation(gate[:, Z], pre_b[:, Z], ACT.Sigmoid).then_inc(z_gate, 1)
                    nc.scalar.activation(keep[:], pre_b[:, Z], ACT.Sigmoid, scale=-1.0).then_inc(z_keep, 1)
                    if not last and t in (2, 3):
                        copy_x(n + BODY, j, t - 2)
                    for half in range(2):
                        act.wait_ge(c_pre[half], now)
                        nc.scalar.activation(gate[:, C, halves(half)], pre_b[:, C, halves(half)], ACT.Tanh)\
                            .then_inc(c_gate[half], 1)

            with act.Fori(0, PASSES - 1) as i:
                for j in range(BODY):
                    block_of_steps(i, j, False)
            for j in range(BODY):
                block_of_steps(PASSES - 1, j, True)

        @block.vector
        def _(dve):
            V = nc.vector
            links = [0]

            def link(ins):
                links[0] += 1
                ins.then_inc(s_link, 1)
                dve.wait_ge(s_link, links[0])

            dve.wait_ge(s_cond_mm, 1)
            V.tensor_copy(cond_t[:], t_bank[:, 0:KD * B].rearrange("p (k b) -> p k b", k=KD)).then_inc(s_cond_t, 1)
            V.tensor_copy(bias_t[:], t_bank[:, KD * B:KD * B + GROUPS]).then_inc(s_cond_t, 1)
            dve.sem_inc(out_ready, 1)
            dve.wait_ge(s_u_in, 16 * G)
            for g in range(G):
                ins = V.tensor_reduce(u_max[:, g:g + 1], u_stage[:, g], AX.XY, ALU.max, apply_absolute_value=True)
            ins.then_inc(s_max, 1)
            dve.wait_ge(s_max_mm, 1)
            link(V.tensor_reduce(top[:], r_bank[0][0:G, 0:P], AX.X, ALU.max))
            link(V.tensor_scalar(power[:].bitcast(i32), top[:].bitcast(i32), 0x7F800000, None, ALU.bitwise_and))
            link(V.tensor_scalar(power[:], power[:], 2.0 ** -60, None, ALU.max))
            V.tensor_scalar(power_diag[:], ident[0:G, 0:G], power[:], None, ALU.mult).then_inc(s_pow, 1)
            dve.wait_ge(s_pow_mm, 1)
            link(V.tensor_copy(powers[:], r_bank[1][:, 0:G]))
            link(V.tensor_scalar(up[:].bitcast(i32), powers[:].bitcast(i32), -1.0, float((254 + UPOW) << 23),
                                 ALU.mult, ALU.add))
            link(V.tensor_scalar(down[:], powers[:], 2.0 ** -UPOW / HSCALE, None, ALU.mult))
            for g in range(G):
                V.tensor_scalar(u_hi[:, g], u_stage[:, g], up[:, g:g + 1], None, ALU.mult).then_inc(s_split, 1)
                dve.wait_ge(s_split, 2 * g + 1)
                V.scalar_tensor_tensor(u_lo[:, g].rearrange("p k e -> p (k e)"),
                                       u_stage[:, g].rearrange("p k e -> p (k e)"), up[:, g:g + 1],
                                       u_hi[:, g].rearrange("p k e -> p (k e)"),
                                       ALU.mult, ALU.subtract).then_inc(s_split, 1)
            dve.wait_ge(s_base_mm, 1)
            dve.wait_ge(s_cond_t, 2)
            V.tensor_tensor(base[:], z_bank[:, 0:GROUPS * B].rearrange("p (q b) -> p q b", q=GROUPS),
                            bias_t[:].unsqueeze(2).to_broadcast([P, GROUPS, B]), ALU.add).then_inc(s_base, 1)
            dve.wait_ge(s_base, 1)

            def take_projection(first, j, q):
                dve.wait_ge(proj_mm, first + q + 1)
                V.tensor_tensor(proj[j][:, q], p_bank[q % 2][:, 0:COLS].rearrange("p (t b) -> p t b", t=TB),
                                base[:, q, :].unsqueeze(1).to_broadcast([P, TB, B]), ALU.add).then_inc(proj_ready, 1)

            def take_result(n, j, u, loads):
                dve.wait_ge(out_turned, NU * n + u + 1)
                if u == 0:
                    dve.wait_ge(result_in[j], loads * 16 * TU)
                V.scalar_tensor_tensor(result[j][:, u], t_bank[:, 0:E], 1.0 / HSCALE, result[j][:, u],
                                       ALU.mult, ALU.add).then_inc(out_ready, 1)

            for q in range(GROUPS):
                take_projection(0, 0, q)

            def add_up(g, j, t, m0, m1, b, part, pre, now):
                s = sums(b, m1 - m0)
                V.scalar_tensor_tensor(pre_a[:, g, m0:m1], s[:, :, 0:B], down[:, g:g + 1],
                                       proj[j][:, g * M + m0:g * M + m1, t, :], ALU.mult, ALU.add).then_inc(part, 1)
                dve.wait_ge(part, now)
                V.scalar_tensor_tensor(pre_b[:, g, m0:m1], s[:, :, B:2 * B], down[:, g:g + 1],
                                       pre_a[:, g, m0:m1], ALU.mult, ALU.add).then_inc(pre, 1)

            PER = GROUPS / TB
            FILL = GROUPS * KD // TB

            def block_of_steps(i, j, last):
                n = i * BODY + j
                fill = not (last and j == BODY - 1)
                first = n * GROUPS + GROUPS if last else dve.snap(n * GROUPS + GROUPS)
                dve.wait_ge(proj_ready, first)
                for t in range(TB):
                    now = n * TB + t + 1 if last else dve.snap(n * TB + t + 1)
                    old = state[:, :, (t - 1) % TB, :]
                    new = state[:, :, t, :]
                    for half in range(2):
                        hm = halves(half)
                        dve.wait_ge(r_mm[half], now)
                        add_up(R, j, t, half * HM, (half + 1) * HM, r_bank[half], r_part[half], r_pre[half], now)
                    for half in range(2):
                        hm = halves(half)
                        dve.wait_ge(r_gate[half], now)
                        V.tensor_tensor(reset_parts[:, hm, 0:B], gate[:, R, hm], old[:, hm], ALU.mult)\
                            .then_inc(rh_hi[half], 1)
                        V.tensor_tensor(reset_full[:, hm], gate[:, R, hm], old[:, hm], ALU.mult)\
                            .then_inc(rh_full[half], 1)
                        dve.wait_ge(rh_hi[half], now)
                        dve.wait_ge(rh_full[half], now)
                        V.tensor_tensor(reset_parts[:, hm, B:2 * B], reset_full[:, hm], reset_parts[:, hm, 0:B],
                                        ALU.subtract).then_inc(rh_lo[half], 1)
                    dve.wait_ge(z_mm, now)
                    add_up(Z, j, t, 0, M, z_bank, z_part, z_pre, now)
                    if t == 4:
                        take_result(n, j, 0, i + 1)
                    dve.wait_ge(z_keep, now)
                    V.tensor_tensor(kept[:], keep[:], old, ALU.mult).then_inc(z_kept, 1)
                    if fill:
                        for q in range(GROUPS):
                            if t * FILL <= q * KD + KD - 1 < t * FILL + FILL // 2:
                                take_projection(first, 1 - j, q)
                    for half in range(2):
                        dve.wait_ge(c_mm[half], now)
                        add_up(C, j, t, half * HM, (half + 1) * HM, c_bank[half], c_part[half], c_pre[half], now)
                    for half in range(2):
                        hm = halves(half)
                        dve.wait_ge(c_gate[half], now)
                        dve.wait_ge(z_gate, now)
                        V.scalar_tensor_tensor(taken[:, hm], gate[:, C, hm], HSCALE, gate[:, Z, hm],
                                               ALU.mult, ALU.mult).then_inc(h_take[half], 1)
                        dve.wait_ge(h_take[half], now)
                        dve.wait_ge(z_kept, now)
                        V.tensor_tensor(state_parts[:, hm, 0:B], taken[:, hm], kept[:, hm], ALU.add)\
                            .then_inc(h_hi[half], 1)
                        V.tensor_tensor(new[:, hm], taken[:, hm], kept[:, hm], ALU.add).then_inc(h_full[half], 1)
                        dve.wait_ge(h_hi[half], now + 1)
                        dve.wait_ge(h_full[half], now)
                        V.tensor_tensor(state_parts[:, hm, B:2 * B], new[:, hm], state_parts[:, hm, 0:B],
                                        ALU.subtract).then_inc(h_lo[half], 1)
                    if fill:
                        for q in range(GROUPS):
                            if t * FILL + FILL // 2 <= q * KD + KD - 1 < (t + 1) * FILL:
                                take_projection(first, 1 - j, q)
                take_result(n, j, 1, i + 1)

            with dve.Fori(0, PASSES - 1) as i:
                for j in range(BODY):
                    block_of_steps(i, j, False)
            for j in range(BODY):
                block_of_steps(PASSES - 1, j, True)


_INS = ["x", "cond_1024", "L0_cond_W_z", "L0_cond_U_z", "L0_cond_C_z", "L0_cond_b_z", "L0_cond_W_r", "L0_cond_U_r",
        "L0_cond_C_r", "L0_cond_b_r", "L0_cond_W", "L0_cond_U", "L0_cond_C", "L0_cond_b"]


def kernel(**inputs):
    import numpy as _np
    import concourse.bacc as _bacc
    from concourse import mybir as _mybir
    from concourse.bass_utils import run_bass_kernel_spmd as _run

    nc = _bacc.Bacc("TRN2", target_bir_lowering=False, num_devices=1)
    arrays, args = {}, []
    for name in _INS:
        a = _np.ascontiguousarray(inputs[name])
        arrays[f"in_{name}_dram"] = a
        args.append(nc.dram_tensor(f"in_{name}_dram", a.shape, _mybir.dt.from_np(a.dtype), kind="ExternalInput").ap())
    shape = inputs["x"].shape
    args.append(nc.dram_tensor("out_dram", shape, _mybir.dt.float32, kind="ExternalOutput").ap())
    conditioned_gru_residual_kernel(nc, *args)
    r = _run(nc, [arrays], core_ids=[0])
    return r.results[0]["out_dram"]
```

```python
import concourse.bass as bass
from concourse import mybir
from contextlib import ExitStack


def conditioned_gru_residual_kernel(nc, x, cond, W_z, U_z, C_z, b_z, W_r, U_r, C_r, b_r, W_h, U_h, C_h, b_h, out):
    f32, f16, bf16, i32 = mybir.dt.float32, mybir.dt.float16, mybir.dt.bfloat16, mybir.dt.int32
    ALU, ACT, AX = mybir.AluOpType, mybir.ActivationFunctionType, mybir.AxisListType

    B, T, D = x.shape
    E = U_z.shape[1]
    P = 128
    KD = D // P
    M = E // P
    G = 3
    R, Z, C = 0, 1, 2
    TU = P // B
    NU = 2
    TB = TU * NU
    COLS = TB * B
    BODY = 2
    BLOCKS = T // TB
    PASSES = BLOCKS // BODY
    GROUPS = G * M
    HM = M // 2
    HSCALE = 2048.0
    POW = 14
    LEAST = 2.0 ** -60
    PARTS = 3
    PRODUCTS = KD * PARTS
    FILL = GROUPS * PRODUCTS // TB
    FILL_Z, FILL_LO = 6, 8
    SQ = 2 * G
    X_SUM, X_TOP, X_TURN, X_LOAD = 0, 1, (2, 3), 4
    assert TB == 8 and X_TURN[-1] < TU
    assert KD == M and P % B == 0 and BLOCKS % BODY == 0

    x_rows = x.rearrange("b (n u t) d -> n t b u d", u=NU, t=TU)
    out_rows = out.rearrange("b (n u t) d -> n t b u d", u=NU, t=TU)

    ctx = ExitStack()
    with ctx:
        def sb(name, shape, dt):
            return ctx.enter_context(nc.sbuf_tensor(name, shape, dt))

        def bank(name):
            return ctx.enter_context(nc.psum_tensor(name, [P, 512], f32))

        def sem(name):
            return ctx.enter_context(nc.semaphore(name))

        def pair(name):
            return [sem(f"{name}{j}") for j in range(2)]

        u_stage = sb("u_stage", [P, G, KD, E], f32)
        c_stage = sb("c_stage", [P, G, KD, E], f32)
        w_stage = sb("w_stage", [P, G, KD, E], f32)
        u_hi = sb("u_hi", [P, G, KD, E], f16)
        u_lo = sb("u_lo", [P, G, KD, E], f16)
        w_hi = sb("w_hi", [P, G, KD, E], f16)
        w_lo = sb("w_lo", [P, G, KD, E], f16)
        x_nat = [sb(f"x_nat{j}", [P, NU, D], f32) for j in range(BODY)]
        x_hi = [sb(f"x_hi{j}", [P, KD, NU, P], f16) for j in range(BODY)]
        x_lo = [sb(f"x_lo{j}", [P, KD, NU, P], f16) for j in range(BODY)]
        x_whole = [sb(f"x_whole{u}", [P, KD, P], f32) for u in range(NU)]
        x_abs = sb("x_abs", [P, D], bf16)
        x_sum = [sb(f"x_sum{j}", [P, NU], f32) for j in range(BODY)]
        x_top = [sb(f"x_top{j}", [P, NU], f32) for j in range(BODY)]
        x_pow = [sb(f"x_pow{j}", [P, 1], f32) for j in range(BODY)]
        x_up = [sb(f"x_up{j}", [P, 1], f32) for j in range(BODY)]
        x_down = [sb(f"x_down{j}", [P, G], f32) for j in range(BODY)]
        proj = [sb(f"proj{j}", [P, GROUPS, TB, B], f32) for j in range(BODY)]
        result = [sb(f"result{j}", [P, NU, E], f32) for j in range(BODY)]
        state = sb("state", [P, M, TB, B], f32)
        state_parts = sb("state_parts", [P, M, 2 * B], f16)
        reset_parts = sb("reset_parts", [P, M, 2 * B], f16)
        reset_full = sb("reset_full", [P, M, B], f32)
        pre_a = sb("pre_a", [P, G, M, B], f32)
        pre_b = sb("pre_b", [P, G, M, B], f32)
        gate = sb("gate", [P, G, M, B], f32)
        keep = sb("keep", [P, M, B], f32)
        kept = sb("kept", [P, M, B], f32)
        taken = sb("taken", [P, M, B], f32)
        ident = sb("ident", [P, P], f32)
        cond_nat = sb("cond_nat", [B, D], f32)
        cond_t = sb("cond_t", [P, KD, B], f32)
        bias_nat = sb("bias_nat", [GROUPS, P], f32)
        bias_t = sb("bias_t", [P, GROUPS], f32)
        base = sb("base", [P, GROUPS, B], f32)
        most = sb("most", [P, SQ], f32)
        top = sb("top", [SQ, 1], f32)
        power = sb("power", [SQ, 1], f32)
        power_diag = sb("power_diag", [SQ, SQ], f32)
        ones = sb("ones", [SQ, P], f32)
        powers = sb("powers", [P, SQ], f32)
        up = sb("up", [P, SQ], f32)
        units = sb("units", [P, G], f32)
        down = sb("down", [P, G], f32)
        down_neg = sb("down_neg", [P, G], f32)
        w_down = sb("w_down", [P, G], f32)

        r_bank, c_bank = [bank("r_bank0"), bank("r_bank1")], [bank("c_bank0"), bank("c_bank1")]
        z_bank = bank("z_bank")
        p_bank = [bank("p_bank0"), bank("p_bank1")]
        t_bank = bank("t_bank")

        def sums(b, blocks):
            return b[:, 0:blocks * 2 * B].rearrange("p (m c) -> p m c", m=blocks)

        def halves(j):
            return slice(j * HM, (j + 1) * HM)

        s_zeroed, s_const = sem("s_zeroed"), sem("s_const")
        s_u_in, s_c_in, s_w_in, s_small_in = sem("s_u_in"), sem("s_c_in"), sem("s_w_in"), sem("s_small_in")
        s_small_turned, s_small_ready = sem("s_small_turned"), sem("s_small_ready")
        s_base_mm, s_most, s_most_turned, s_power, s_power_mm = (
            sem(n) for n in ("s_base_mm", "s_most", "s_most_turned", "s_power", "s_power_mm"))
        s_link, s_split, s_units = sem("s_link"), sem("s_split"), sem("s_units")
        x_in, result_in, result_out = pair("x_in"), pair("result_in"), pair("result_out")
        x_sum_ready, x_top_ready, x_link = sem("x_sum_ready"), sem("x_top_ready"), sem("x_link")
        x_scale, x_turned, x_hi_ready, x_t_ready = (sem(n) for n in ("x_scale", "x_turned", "x_hi_ready", "x_t_ready"))
        x_whole_ready = sem("x_whole_ready")
        proj_mm, proj_ready = sem("proj_mm"), sem("proj_ready")
        out_turned, out_ready = sem("out_turned"), sem("out_ready")
        r_mm, z_mm, c_mm = pair("r_mm"), sem("z_mm"), pair("c_mm")
        r_part, r_pre, r_gate = pair("r_part"), pair("r_pre"), pair("r_gate")
        rh_hi, rh_full, rh_lo = pair("rh_hi"), pair("rh_full"), pair("rh_lo")
        z_part, z_pre, z_keep, z_kept = (sem(n) for n in ("z_part", "z_pre", "z_keep", "z_kept"))
        c_part, c_pre, c_gate = pair("c_part"), pair("c_pre"), pair("c_gate")
        h_take, h_hi, h_full, h_lo = pair("h_take"), pair("h_hi"), pair("h_full"), pair("h_lo")

        block = ctx.enter_context(nc.Block())

        @block.sync
        def _(sp):
            def load_x(n, j, buffers, done):
                for t in range(TU):
                    sp.dma_start(buffers[j][t * B:(t + 1) * B], x_rows[n, t]).then_inc(done[j], 16)

            for g, w in enumerate((W_r, W_z, W_h)):
                sp.dma_start(w_stage[:, g], w.rearrange("(k p) e -> p k e", p=P)).then_inc(s_w_in, 16)
            for g, u in enumerate((U_r, U_z, U_h)):
                sp.dma_start(u_stage[:, g], u.rearrange("(k p) e -> p k e", p=P)).then_inc(s_u_in, 16)
            for g, c in enumerate((C_r, C_z, C_h)):
                sp.dma_start(c_stage[:, g], c.rearrange("(k p) e -> p k e", p=P)).then_inc(s_c_in, 16)
            for j in range(BODY):
                load_x(j, j, result, result_in)

            def block_of_steps(i, j, last):
                n = i * BODY + j
                tiles = NU * n + NU + 2 if last else sp.snap(NU * n + NU + 2)
                sp.wait_ge(out_ready, tiles)
                for t in range(TU):
                    sp.dma_start(out_rows[n, t], result[j][t * B:(t + 1) * B]).then_inc(result_out[j], 16)
                sp.wait_ge(result_out[j], (i + 1) * 16 * TU)
                if not last:
                    load_x(n + BODY, j, result, result_in)

            with sp.Fori(0, PASSES - 1) as i:
                for j in range(BODY):
                    block_of_steps(i, j, False)
            for j in range(BODY):
                block_of_steps(PASSES - 1, j, True)

        @block.gpsimd
        def _(pool):
            nc.gpsimd.memset(ident[:], 0.0).then_inc(s_zeroed, 1)
            nc.gpsimd.memset(ones[:], 1.0).then_inc(s_const, 1)
            nc.gpsimd.memset(state[:], 0.0).then_inc(s_const, 1)
            nc.gpsimd.memset(state_parts[:], 0.0).then_inc(s_const, 1)
            pool.wait_ge(s_const, 3)
            for j in range(2):
                pool.sem_inc(h_hi[j], 1)
                pool.sem_inc(h_lo[j], 1)
            pool.wait_ge(s_zeroed, 1)
            nc.gpsimd.affine_select(out=ident[:], in_=ident[:], compare_op=ALU.not_equal, fill=1.0, base=0,
                                    pattern=[[-1, P]], channel_multiplier=1).then_inc(s_const, 1)

            def top_of_x(n, j):
                nc.gpsimd.partition_all_reduce(x_top[j][:], x_sum[j][:], P, bass.bass_isa.ReduceOp.max)\
                    .then_inc(x_top_ready, 1)

            def x_rest(n, u):
                nc.gpsimd.tensor_tensor(x_lo[n][:, :, u, :], x_whole[u][:], x_hi[n][:, :, u, :], ALU.subtract)\
                    .then_inc(x_t_ready, 1)

            for n in range(BODY):
                pool.wait_ge(x_sum_ready, NU * n + NU)
                top_of_x(n, n)
            for n in range(BODY):
                for u in range(NU):
                    pool.wait_ge(x_hi_ready, NU * n + u + 1)
                    x_rest(n, u)

            def block_of_steps(i, j, last):
                n = i * BODY + j
                for t in range(TB):
                    now = n * TB + t + 1 if last else pool.snap(n * TB + t + 1)
                    old = state[:, :, (t - 1) % TB, :]
                    for half in range(2):
                        hm = halves(half)
                        pool.wait_ge(r_gate[half], now)
                        nc.gpsimd.tensor_tensor(reset_full[:, hm], gate[:, R, hm], old[:, hm], ALU.mult)\
                            .then_inc(rh_full[half], 1)
                    if not last and t == X_TOP:
                        pool.wait_ge(x_sum_ready, NU * n + NU * BODY + NU)
                    for half in range(2):
                        hm = halves(half)
                        pool.wait_ge(rh_full[half], now)
                        pool.wait_ge(rh_hi[half], now)
                        nc.gpsimd.tensor_tensor(reset_parts[:, hm, B:2 * B], reset_full[:, hm],
                                                reset_parts[:, hm, 0:B], ALU.subtract).then_inc(rh_lo[half], 1)
                    if not last and t == X_TOP:
                        top_of_x(n + BODY, j)
                    if not last and t - 1 in X_TURN:
                        u = X_TURN.index(t - 1)
                        pool.wait_ge(x_hi_ready, NU * n + NU * BODY + u + 1)
                        x_rest(j, u)

            with pool.Fori(0, PASSES - 1) as i:
                for j in range(BODY):
                    block_of_steps(i, j, False)
            for j in range(BODY):
                block_of_steps(PASSES - 1, j, True)

        @block.tensor
        def _(pe):
            pe.wait_ge(s_const, 4)
            pe.wait_ge(s_small_in, 16 * (1 + G))
            for k in range(KD):
                nc.tensor.transpose(t_bank[:, k * B:(k + 1) * B], cond_nat[:, k * P:(k + 1) * P], ident[0:B, 0:B])
            nc.tensor.transpose(t_bank[:, KD * B:KD * B + GROUPS], bias_nat[:], ident[0:GROUPS, 0:GROUPS])\
                .then_inc(s_small_turned, 1)

            def turn(tiles):
                for k, tile in enumerate(tiles):
                    last = nc.tensor.transpose(t_bank[:, k * P:(k + 1) * P], tile, ident[:])
                return last

            def turn_x(j, u):
                turn([x_nat[j][:, u, k * P:(k + 1) * P] for k in range(KD)]).then_inc(x_turned, 1)

            def turn_state(u):
                turn([state[:, m, u * TU:(u + 1) * TU, :] for m in range(M)]).then_inc(out_turned, 1)

            def project(first, j, f0, f1):
                for f in range(f0, f1):
                    q, c = divmod(f, PRODUCTS)
                    k, c = divmod(c, PARTS)
                    g, m = divmod(q, M)
                    if k == 0 and c == 0 and not (q < 2 and isinstance(first, int) and first == 0):
                        pe.wait_ge(proj_ready, first + (q - 1))
                    w, xs = ((w_hi, x_hi), (w_hi, x_lo), (w_lo, x_hi))[c]
                    last = nc.tensor.matmul(p_bank[q % 2][:, 0:COLS], w[:, g, k, m * P:(m + 1) * P],
                                            xs[j][:, k, :, :], start=(k == 0 and c == 0),
                                            stop=(k == KD - 1 and c == PARTS - 1))
                    if k == KD - 1 and c == PARTS - 1:
                        last.then_inc(proj_mm, 1)

            def times_u_lo(g, banks, parts, hi_ready, now, which=((0, 0, M), (1, 0, M))):
                per = M // len(banks)
                for half, m0, m1 in which:
                    pe.wait_ge(hi_ready[half], now)
                    for m in range(m0, m1):
                        for k in range(half * HM, (half + 1) * HM):
                            nc.tensor.matmul(sums(banks[m // per], per)[:, m % per, 0:B],
                                             u_lo[:, g, k, m * P:(m + 1) * P], parts[:, k, 0:B],
                                             start=(half == 0 and k == 0 and m % per == 0), stop=False,
                                             skip_group_check=True)

            def times_u_hi(g, banks, parts, lo_ready, now, done):
                per = M // len(banks)
                for half in range(2):
                    pe.wait_ge(lo_ready[half], now)
                    for m in range(M):
                        for k in range(half * HM, (half + 1) * HM):
                            last = nc.tensor.matmul(sums(banks[m // per], per)[:, m % per, :],
                                                    u_hi[:, g, k, m * P:(m + 1) * P], parts[:, k, :],
                                                    start=False, stop=(k == KD - 1), skip_group_check=True)
                        if half == 1 and m % per == per - 1:
                            last.then_inc(done[m // per], 1)

            pe.wait_ge(s_most, 1)
            nc.tensor.transpose(r_bank[0][0:SQ, 0:P], most[:], ident[:]).then_inc(s_most_turned, 1)
            pe.wait_ge(s_power, 1)
            nc.tensor.matmul(r_bank[1][:, 0:SQ], ones[:], power_diag[:], start=True, stop=True).then_inc(s_power_mm, 1)
            pe.wait_ge(s_small_ready, 1)
            pe.wait_ge(s_c_in, 16 * G)
            for q in range(GROUPS):
                g, m = divmod(q, M)
                for k in range(KD):
                    last = nc.tensor.matmul(z_bank[:, q * B:(q + 1) * B], c_stage[:, g, k, m * P:(m + 1) * P],
                                            cond_t[:, k, :], start=(k == 0), stop=(k == KD - 1))
            last.then_inc(s_base_mm, 1)
            for n in range(BODY):
                pe.wait_ge(x_in[n], 16 * TU)
                for u in range(NU):
                    if n + u:
                        pe.wait_ge(x_hi_ready, NU * n + u)
                    turn_x(n, u)
            pe.wait_ge(s_split, 2 * SQ)
            pe.wait_ge(x_t_ready, NU)
            project(0, 0, 0, GROUPS * PRODUCTS)

            def block_of_steps(i, j, last):
                n = i * BODY + j
                fill = not (last and j == BODY - 1)
                first = n * GROUPS + GROUPS if last else pe.snap(n * GROUPS + GROUPS)
                for t in range(TB):
                    now = n * TB + t + 1 if last else pe.snap(n * TB + t + 1)
                    times_u_lo(R, r_bank, state_parts, h_hi, now)
                    times_u_lo(Z, [z_bank], state_parts, h_hi, now, [(0, 0, HM)])
                    times_u_hi(R, r_bank, state_parts, h_lo, now, r_mm)
                    times_u_lo(Z, [z_bank], state_parts, h_hi, now, [(0, HM, M), (1, 0, M)])
                    times_u_hi(Z, [z_bank], state_parts, h_lo, now, [z_mm])
                    if t == 0:
                        pe.wait_ge(x_hi_ready, BLOCKS * NU if last else NU * n + NU * BODY)
                        pe.wait_ge(out_ready, NU * n + 1)
                        turn_state(1)
                    if t == TU:
                        if last:
                            pe.wait_ge(out_ready, NU * n + 2)
                        pe.wait_ge(x_hi_ready, BLOCKS * NU if last else NU * n + NU * BODY + NU)
                        turn_state(0)
                    if fill:
                        if t == 0:
                            pe.wait_ge(x_t_ready, NU * n + 2 * NU)
                        project(first, 1 - j, t * FILL, t * FILL + FILL_Z)
                    times_u_lo(C, c_bank, reset_parts, rh_hi, now)
                    if fill:
                        project(first, 1 - j, t * FILL + FILL_Z, t * FILL + FILL_LO)
                    times_u_hi(C, c_bank, reset_parts, rh_lo, now, c_mm)
                    if not last and t in X_TURN:
                        u = X_TURN.index(t)
                        if u == 0:
                            pe.wait_ge(out_ready, NU * n + 2)
                            pe.wait_ge(x_in[j], (i + 2) * 16 * TU)
                        else:
                            pe.wait_ge(x_hi_ready, NU * n + NU * BODY + u)
                        turn_x(j, u)
                    if fill:
                        project(first, 1 - j, t * FILL + FILL_LO, (t + 1) * FILL)

            with pe.Fori(0, PASSES - 1) as i:
                for j in range(BODY):
                    block_of_steps(i, j, False)
            for j in range(BODY):
                block_of_steps(PASSES - 1, j, True)
            for half in range(2):
                pe.wait_ge(h_full[half], T)
            pe.wait_ge(out_ready, BLOCKS * NU + 1)
            turn_state(1)

        @block.scalar
        def _(act):
            act.dma_start(cond_nat[:], cond).then_inc(s_small_in, 16)
            for g, b in enumerate((b_r, b_z, b_h)):
                act.dma_start(bias_nat[g * M:(g + 1) * M], b.rearrange("(m p) -> m p", p=P)).then_inc(s_small_in, 16)
            for j in range(BODY):
                for t in range(TU):
                    act.dma_start(x_nat[j][t * B:(t + 1) * B], x_rows[j, t]).then_inc(x_in[j], 16)

            def sum_x(j, u):
                nc.scalar.activation(x_abs[:], x_nat[j][:, u], ACT.Abs, accum_out=x_sum[j][:, u:u + 1])\
                    .then_inc(x_sum_ready, 1)

            def copy_x(n, j, u):
                act.wait_ge(x_turned, NU * n + u + 1)
                tile = t_bank[:, 0:KD * P].rearrange("p (k c) -> p k c", k=KD)
                nc.scalar.activation(x_whole[u][:], tile, ACT.Copy, scale=x_up[j][:]).then_inc(x_whole_ready, 1)
                nc.scalar.activation(x_hi[j][:, :, u, :], tile, ACT.Copy, scale=x_up[j][:]).then_inc(x_hi_ready, 1)

            def load_x(n, j):
                for t in range(TU):
                    act.dma_start(x_nat[j][t * B:(t + 1) * B], x_rows[n, t]).then_inc(x_in[j], 16)

            for n in range(BODY):
                act.wait_ge(x_in[n], 16 * TU)
                for u in range(NU):
                    if n + u:
                        act.wait_ge(x_sum_ready, NU * n + u)
                    sum_x(n, u)
            for n in range(BODY):
                act.wait_ge(x_scale, n + 1)
                for u in range(NU):
                    if n > 0:
                        act.wait_ge(x_t_ready, NU * (n - 1) + u + 1)
                    copy_x(n, n, u)
                load_x(n + BODY, n)
            act.wait_ge(s_units, 1)
            scales = []
            for name, scale in (("r", down[0:1, R:R + 1]), ("z", down[0:1, Z:Z + 1]), ("c", down[0:1, C:C + 1]),
                                ("keep", down_neg[0:1, Z:Z + 1])):
                scales.append(act.alloc_register(f"scale_{name}"))
                act.reg_load(scales[-1], scale.bitcast(i32))
            scale_r, scale_z, scale_c, scale_keep = scales

            def block_of_steps(i, j, last):
                n = i * BODY + j
                for t in range(TB):
                    now = n * TB + t + 1 if last else act.snap(n * TB + t + 1)
                    for half in range(2):
                        act.wait_ge(r_pre[half], now)
                        nc.scalar.activation(gate[:, R, halves(half)], pre_b[:, R, halves(half)], ACT.Sigmoid,
                                             scale=scale_r).then_inc(r_gate[half], 1)
                    act.wait_ge(z_pre, now)
                    nc.scalar.activation(keep[:], pre_b[:, Z], ACT.Sigmoid, scale=scale_keep)\
                        .then_inc(z_keep, 1)
                    nc.scalar.activation(gate[:, Z], pre_b[:, Z], ACT.Sigmoid, scale=scale_z)
                    for half in range(2):
                        act.wait_ge(c_pre[half], now)
                        nc.scalar.activation(gate[:, C, halves(half)], pre_b[:, C, halves(half)], ACT.Tanh,
                                             scale=scale_c).then_inc(c_gate[half], 1)
                    if not last and t == X_SUM:
                        act.wait_ge(x_in[j], (i + 2) * 16 * TU)
                        for u in range(NU):
                            act.wait_ge(x_sum_ready, NU * (n + BODY) + u)
                            sum_x(j, u)
                    if not last and t in X_TURN:
                        u = X_TURN.index(t)
                        if u == 0:
                            act.wait_ge(x_scale, n + BODY + 1)
                        act.wait_ge(x_t_ready, NU * (n + BODY - 1) + u + 1)
                        copy_x(n + BODY, j, u)
                    if not last and t == X_LOAD:
                        load_x((n + 2 * BODY) % BLOCKS, j)

            with act.Fori(0, PASSES - 1) as i:
                for j in range(BODY):
                    block_of_steps(i, j, False)
            for j in range(BODY):
                block_of_steps(PASSES - 1, j, True)
            for j in range(BODY):
                act.wait_ge(x_in[j], (PASSES + 1) * 16 * TU)

        @block.vector
        def _(dve):
            V = nc.vector
            links = [0]

            def link(ins):
                links[0] += 1
                ins.then_inc(s_link, 1)
                dve.wait_ge(s_link, links[0])

            dve.wait_ge(s_small_turned, 1)
            V.tensor_copy(bias_t[:], t_bank[:, KD * B:KD * B + GROUPS]).then_inc(s_link, 1)
            V.tensor_copy(cond_t[:], t_bank[:, 0:KD * B].rearrange("p (k b) -> p k b", k=KD)).then_inc(s_link, 1)
            links[0] = 2
            dve.wait_ge(s_link, 2)
            dve.sem_inc(s_small_ready, 1)
            dve.sem_inc(out_ready, 1)

            def power_of(out_, in_):
                link(V.tensor_scalar(out_.bitcast(i32), in_.bitcast(i32), 0x7F800000, None, ALU.bitwise_and))
                link(V.tensor_scalar(out_, out_, LEAST, None, ALU.max))

            def scale_of(out_, power_, pow_):
                return V.tensor_scalar(out_.bitcast(i32), power_.bitcast(i32), -1.0, float((254 + pow_) << 23),
                                       ALU.mult, ALU.add)

            for g in (3, 4, 5, 0, 1, 2):
                if g % G == 0:
                    dve.wait_ge((s_u_in, s_w_in)[g // G], 16 * G)
                ins = V.tensor_reduce(most[:, g:g + 1], (u_stage, w_stage)[g // G][:, g % G], AX.XY, ALU.max,
                                      apply_absolute_value=True)
            ins.then_inc(s_most, 1)
            dve.wait_ge(s_most_turned, 1)
            link(V.tensor_reduce(top[:], r_bank[0][0:SQ, 0:P], AX.X, ALU.max))
            power_of(power[:], top[:])
            V.tensor_scalar(power_diag[:], ident[0:SQ, 0:SQ], power[:], None, ALU.mult).then_inc(s_power, 1)
            dve.wait_ge(s_power_mm, 1)
            link(V.tensor_copy(powers[:], r_bank[1][:, 0:SQ]))
            link(scale_of(up[:], powers[:], POW))
            link(V.tensor_scalar(units[:], up[:, 0:G], HSCALE, None, ALU.mult))
            link(V.tensor_scalar(down[:], powers[:, 0:G], 2.0 ** -POW / HSCALE, None, ALU.mult))
            V.tensor_scalar(down_neg[:], down[:], -1.0, None, ALU.mult).then_inc(s_units, 1)
            link(V.scalar_tensor_tensor(w_down[:], powers[:, G:SQ], 2.0 ** (-2 * POW), units[:], ALU.mult, ALU.mult))

            def split(stage, hi, lo, g, scale, count):
                V.tensor_scalar(hi[:, g], stage[:, g], scale, None, ALU.mult).then_inc(s_split, 1)
                dve.wait_ge(s_split, count)
                V.scalar_tensor_tensor(lo[:, g].rearrange("p k e -> p (k e)"), stage[:, g].rearrange("p k e -> p (k e)"),
                                       scale, hi[:, g].rearrange("p k e -> p (k e)"),
                                       ALU.mult, ALU.subtract).then_inc(s_split, 1)

            for g in range(G):
                split(w_stage, w_hi, w_lo, g, up[:, G + g:G + g + 1], 4 * g + 1)
                split(u_stage, u_hi, u_lo, g, up[:, g:g + 1], 4 * g + 3)
            dve.wait_ge(s_base_mm, 1)
            link(V.tensor_tensor(base[:], z_bank[:, 0:GROUPS * B].rearrange("p (q b) -> p q b", q=GROUPS),
                                 bias_t[:].unsqueeze(2).to_broadcast([P, GROUPS, B]), ALU.add))
            for g in range(G):
                ins = V.tensor_scalar(base[:, g * M:(g + 1) * M], base[:, g * M:(g + 1) * M], units[:, g:g + 1], None,
                                      ALU.mult)
            link(ins)

            def x_scale_step(n, j, c):
                if c:
                    dve.wait_ge(x_link, 3 * n + c)
                if c == 0:
                    dve.wait_ge(x_top_ready, n + 1)
                    V.tensor_reduce(x_pow[j][:], x_top[j][:], AX.X, ALU.max).then_inc(x_link, 1)
                elif c == 1:
                    V.tensor_scalar(x_pow[j][:].bitcast(i32), x_pow[j][:].bitcast(i32), 0x7F800000, None,
                                    ALU.bitwise_and).then_inc(x_link, 1)
                elif c == 2:
                    V.tensor_scalar(x_pow[j][:], x_pow[j][:], LEAST, None, ALU.max).then_inc(x_link, 1)
                else:
                    V.tensor_scalar(x_down[j][:], w_down[:], x_pow[j][:], None, ALU.mult)
                    scale_of(x_up[j][:], x_pow[j][:], POW).then_inc(x_scale, 1)

            def take_projection(first, j, q):
                dve.wait_ge(proj_mm, first + q + 1)
                V.scalar_tensor_tensor(proj[j][:, q], p_bank[q % 2][:, 0:COLS].rearrange("p (t b) -> p t b", t=TB),
                                       x_down[j][:, q // M:q // M + 1],
                                       base[:, q, :].unsqueeze(1).to_broadcast([P, TB, B]),
                                       ALU.mult, ALU.add).then_inc(proj_ready, 1)

            def take_result(j, u, e0, e1):
                ins = V.scalar_tensor_tensor(result[j][:, u, e0:e1], t_bank[:, e0:e1], 1.0 / HSCALE,
                                             result[j][:, u, e0:e1], ALU.mult, ALU.add)
                if e1 == E:
                    ins.then_inc(out_ready, 1)

            for n in range(BODY):
                for c in range(4):
                    x_scale_step(n, n, c)
            dve.wait_ge(x_scale, BODY)
            dve.wait_ge(result_in[1], 16 * TU)
            for q in range(GROUPS):
                take_projection(0, 0, q)

            def add_hi(g, j, t, m0, m1, b, part):
                V.tensor_tensor(pre_a[:, g, m0:m1], sums(b, m1 - m0)[:, :, 0:B],
                                proj[j][:, g * M + m0:g * M + m1, t, :], ALU.add).then_inc(part, 1)

            def add_lo(g, m0, m1, b, part, pre, now):
                dve.wait_ge(part, now)
                V.tensor_tensor(pre_b[:, g, m0:m1], sums(b, m1 - m0)[:, :, B:2 * B], pre_a[:, g, m0:m1],
                                ALU.add).then_inc(pre, 1)

            def block_of_steps(i, j, last):
                n = i * BODY + j
                fill = not (last and j == BODY - 1)
                first = n * GROUPS + GROUPS if last else dve.snap(n * GROUPS + GROUPS)
                dve.wait_ge(proj_ready, first)

                def projections(f0, f1):
                    for q in range(GROUPS):
                        if fill and f0 <= q * PRODUCTS + PRODUCTS - 1 < f1:
                            take_projection(first, 1 - j, q)

                for t in range(TB):
                    now = n * TB + t + 1 if last else dve.snap(n * TB + t + 1)
                    old = state[:, :, (t - 1) % TB, :]
                    new = state[:, :, t, :]
                    for half in range(2):
                        dve.wait_ge(r_mm[half], now)
                        add_hi(R, j, t, half * HM, (half + 1) * HM, r_bank[half], r_part[half])
                    for half in range(2):
                        add_lo(R, half * HM, (half + 1) * HM, r_bank[half], r_part[half], r_pre[half], now)
                    for half in range(2):
                        hm = halves(half)
                        dve.wait_ge(r_gate[half], now)
                        V.tensor_tensor(reset_parts[:, hm, 0:B], gate[:, R, hm], old[:, hm], ALU.mult)\
                            .then_inc(rh_hi[half], 1)
                    if not last and t == X_TOP + 1:
                        x_scale_step(n + BODY, j, 1)
                    dve.wait_ge(z_mm, now)
                    add_hi(Z, j, t, 0, M, z_bank, z_part)
                    add_lo(Z, 0, M, z_bank, z_part, z_pre, now)
                    if t == 0:
                        dve.wait_ge(out_turned, NU * n + 1)
                        take_result(1 - j, 1, 0, E // 2)
                    if t == 2:
                        take_result(1 - j, 1, E // 2, E)
                    if t == TU:
                        dve.wait_ge(result_in[j], (i + 1) * 16 * TU)
                        dve.wait_ge(out_turned, NU * n + 2)
                        take_result(j, 0, 0, E // 2)
                    if t == TU + 2:
                        take_result(j, 0, E // 2, E)
                    if not last and t == X_TOP + 1:
                        x_scale_step(n + BODY, j, 2)
                    projections(t * FILL, t * FILL + FILL_Z)
                    dve.wait_ge(z_keep, now)
                    V.tensor_tensor(kept[:], keep[:], old, ALU.mult).then_inc(z_kept, 1)
                    if not last and t == X_TOP + 1:
                        x_scale_step(n + BODY, j, 3)
                    for half in range(2):
                        dve.wait_ge(c_mm[half], now)
                        add_hi(C, j, t, half * HM, (half + 1) * HM, c_bank[half], c_part[half])
                    for half in range(2):
                        add_lo(C, half * HM, (half + 1) * HM, c_bank[half], c_part[half], c_pre[half], now)
                    dve.wait_ge(z_kept, now)
                    for half in range(2):
                        hm = halves(half)
                        dve.wait_ge(c_gate[half], now)
                        V.scalar_tensor_tensor(taken[:, hm], gate[:, C, hm], HSCALE, gate[:, Z, hm],
                                               ALU.mult, ALU.mult).then_inc(h_take[half], 1)
                    for half in range(2):
                        hm = halves(half)
                        dve.wait_ge(h_take[half], now)
                        V.tensor_tensor(state_parts[:, hm, 0:B], taken[:, hm], kept[:, hm], ALU.add)\
                            .then_inc(h_hi[half], 1)
                    for half in range(2):
                        hm = halves(half)
                        V.tensor_tensor(new[:, hm], taken[:, hm], kept[:, hm], ALU.add).then_inc(h_full[half], 1)
                    for half in range(2):
                        hm = halves(half)
                        dve.wait_ge(h_full[half], now)
                        V.tensor_tensor(state_parts[:, hm, B:2 * B], new[:, hm], state_parts[:, hm, 0:B],
                                        ALU.subtract).then_inc(h_lo[half], 1)
                    if not last and t == X_TOP:
                        x_scale_step(n + BODY, j, 0)
                    projections(t * FILL + FILL_LO, (t + 1) * FILL)

            with dve.Fori(0, PASSES - 1) as i:
                for j in range(BODY):
                    block_of_steps(i, j, False)
            for j in range(BODY):
                block_of_steps(PASSES - 1, j, True)
            dve.wait_ge(out_turned, BLOCKS * NU + 1)
            take_result(BODY - 1, 1, 0, E)


_INS = ["x", "cond_1024", "L0_cond_W_z", "L0_cond_U_z", "L0_cond_C_z", "L0_cond_b_z", "L0_cond_W_r", "L0_cond_U_r",
        "L0_cond_C_r", "L0_cond_b_r", "L0_cond_W", "L0_cond_U", "L0_cond_C", "L0_cond_b"]


def kernel(**inputs):
    import numpy as _np
    import concourse.bacc as _bacc
    from concourse import mybir as _mybir
    from concourse.bass_utils import run_bass_kernel_spmd as _run

    nc = _bacc.Bacc("TRN2", target_bir_lowering=False, num_devices=1)
    arrays, args = {}, []
    for name in _INS:
        a = _np.ascontiguousarray(inputs[name])
        arrays[f"in_{name}_dram"] = a
        args.append(nc.dram_tensor(f"in_{name}_dram", a.shape, _mybir.dt.from_np(a.dtype), kind="ExternalInput").ap())
    shape = inputs["x"].shape
    args.append(nc.dram_tensor("out_dram", shape, _mybir.dt.float32, kind="ExternalOutput").ap())
    conditioned_gru_residual_kernel(nc, *args)
    r = _run(nc, [arrays], core_ids=[0])
    return r.results[0]["out_dram"]
```

```python
import concourse.bass as bass
from concourse import mybir
from contextlib import ExitStack


def conditioned_gru_residual_kernel(nc, x, cond, W_z, U_z, C_z, b_z, W_r, U_r, C_r, b_r, W_h, U_h, C_h, b_h, out):
    f32, f16, bf16, i32 = mybir.dt.float32, mybir.dt.float16, mybir.dt.bfloat16, mybir.dt.int32
    ALU, ACT, AX = mybir.AluOpType, mybir.ActivationFunctionType, mybir.AxisListType

    B, T, D = x.shape
    E = U_z.shape[1]
    P = 128
    KD = D // P
    M = E // P
    G = 3
    R, Z, C = 0, 1, 2
    TU = P // B
    NU = 2
    TB = TU * NU
    COLS = TB * B
    BODY = 2
    BLOCKS = T // TB
    PASSES = BLOCKS // BODY
    GROUPS = G * M
    HM = M // 2
    HSCALE = 2048.0
    POW = 14
    LEAST = 2.0 ** -60
    PARTS = 3
    PRODUCTS = KD * PARTS
    FILLS = (16, 20, 20, 16, 16, 17, 20, 19)
    H_TURN = (0, 5)
    H_ROWS = (1, 6)
    BEFORE_C = [3 if t in H_TURN else 7 for t in range(TB)]
    START = [sum(FILLS[:t]) for t in range(TB + 1)]
    assert TB == 8 and START[TB] == GROUPS * PRODUCTS
    R_ORDER = ((0, 0), (0, 1), (1, 0), (1, 1))
    C_ORDER = ((0, 0), (1, 0), (0, 1), (1, 1))
    X_SUM, X_TOP, X_TURN, X_LOAD = 0, 1, (3, 4), 5
    X_SCALE_EARLY, X_SCALE_LATE = {3: (3,)}, {1: (0, 1), 2: (2,)}
    assert KD == M and P % B == 0 and BLOCKS % BODY == 0

    takes, q = [], 0
    for t in range(TB):
        for end in (START[t] + BEFORE_C[t], START[t + 1]):
            ready = q < GROUPS and (q + 1) * PRODUCTS <= end
            takes.append([q] if ready else [])
            q += len(takes[-1])
    assert q == GROUPS

    x_rows = x.rearrange("b (n u t) d -> n t b u d", u=NU, t=TU)
    out_rows = out.rearrange("b (n u t) d -> n t b u d", u=NU, t=TU)

    ctx = ExitStack()
    with ctx:
        def sb(name, shape, dt):
            return ctx.enter_context(nc.sbuf_tensor(name, shape, dt))

        def bank(name):
            return ctx.enter_context(nc.psum_tensor(name, [P, 512], f32))

        def sem(name):
            return ctx.enter_context(nc.semaphore(name))

        def pair(name):
            return [sem(f"{name}{j}") for j in range(2)]

        u_stage = sb("u_stage", [P, G, KD, E], f32)
        c_stage = sb("c_stage", [P, G, KD, E], f32)
        w_stage = sb("w_stage", [P, G, KD, E], f32)
        u_hi = sb("u_hi", [P, G, KD, E], f16)
        u_lo = sb("u_lo", [P, G, KD, E], f16)
        w_hi = sb("w_hi", [P, G, KD, E], f16)
        w_lo = sb("w_lo", [P, G, KD, E], f16)
        x_nat = [sb(f"x_nat{j}", [P, NU, D], f32) for j in range(BODY)]
        x_hi = [sb(f"x_hi{j}", [P, KD, NU, P], f16) for j in range(BODY)]
        x_lo = [sb(f"x_lo{j}", [P, KD, NU, P], f16) for j in range(BODY)]
        x_whole = [sb(f"x_whole{u}", [P, KD, P], f32) for u in range(NU)]
        x_abs = sb("x_abs", [P, D], bf16)
        x_sum = [sb(f"x_sum{j}", [P, NU], f32) for j in range(BODY)]
        x_top = [sb(f"x_top{j}", [P, NU], f32) for j in range(BODY)]
        x_pow = [sb(f"x_pow{j}", [P, 1], f32) for j in range(BODY)]
        x_up = [sb(f"x_up{j}", [P, 1], f32) for j in range(BODY)]
        x_down = [sb(f"x_down{j}", [P, G], f32) for j in range(BODY)]
        proj = [sb(f"proj{j}", [P, GROUPS, TB, B], f32) for j in range(BODY)]
        result = [sb(f"result{j}", [P, NU, E], f32) for j in range(BODY)]
        h_rows = sb("h_rows", [P, E], f32)
        state = sb("state", [P, M, TB, B], f32)
        state_parts = sb("state_parts", [P, M, 2 * B], f16)
        reset_parts = sb("reset_parts", [P, M, 2 * B], f16)
        reset_full = sb("reset_full", [P, M, B], f32)
        pre_a = sb("pre_a", [P, G, M, B], f32)
        pre_b = sb("pre_b", [P, G, M, B], f32)
        gate = sb("gate", [P, G, M, B], f32)
        keep = sb("keep", [P, M, B], f32)
        kept = sb("kept", [P, M, B], f32)
        taken = sb("taken", [P, M, B], f32)
        ident = sb("ident", [P, P], f32)
        cond_nat = sb("cond_nat", [B, D], f32)
        cond_t = sb("cond_t", [P, KD, B], f32)
        bias_nat = sb("bias_nat", [GROUPS, P], f32)
        bias_t = sb("bias_t", [P, GROUPS], f32)
        base = sb("base", [P, GROUPS, B], f32)
        u_sum = [sb(f"u_sum{g}", [P, 1], f32) for g in range(G)]
        w_sum = [sb(f"w_sum{g}", [P, 1], f32) for g in range(G)]
        u_top = [sb(f"u_top{g}", [P, 1], f32) for g in range(G)]
        w_top = [sb(f"w_top{g}", [P, 1], f32) for g in range(G)]
        u_pow, w_pow = sb("u_pow", [P, G], f32), sb("w_pow", [P, G], f32)
        u_up, w_up = sb("u_up", [P, G], f32), sb("w_up", [P, G], f32)
        units = sb("units", [P, G], f32)
        down = sb("down", [P, G], f32)
        down_neg = sb("down_neg", [P, G], f32)
        w_down = sb("w_down", [P, G], f32)

        r_bank, c_bank = [bank("r_bank0"), bank("r_bank1")], [bank("c_bank0"), bank("c_bank1")]
        z_bank = bank("z_bank")
        p_bank = [bank("p_bank0"), bank("p_bank1")]
        base_bank = [*r_bank, c_bank[0]]
        t_bank = bank("t_bank")

        def sums(b, blocks):
            return b[:, 0:blocks * 2 * B].rearrange("p (m c) -> p m c", m=blocks)

        def halves(j):
            return slice(j * HM, (j + 1) * HM)

        s_zeroed, s_const = sem("s_zeroed"), sem("s_const")
        s_small_in = sem("s_small_in")
        s_c_in, s_w_in, s_u_in = ([sem(f"{n}{g}") for g in range(G)] for n in ("s_c_in", "s_w_in", "s_u_in"))
        s_small_turned, s_small_ready = sem("s_small_turned"), sem("s_small_ready")
        s_base_mm, s_link, s_units = sem("s_base_mm"), sem("s_link"), sem("s_units")
        s_w_sum, s_w_top, s_w_scale, s_w_hi, s_w_split = (
            sem(n) for n in ("s_w_sum", "s_w_top", "s_w_scale", "s_w_hi", "s_w_split"))
        s_u_sum, s_u_top, s_u_scale, s_u_hi, s_u_split = (
            sem(n) for n in ("s_u_sum", "s_u_top", "s_u_scale", "s_u_hi", "s_u_split"))
        x_in, result_in, result_out = pair("x_in"), pair("result_in"), pair("result_out")
        x_sum_ready, x_top_ready, x_link = sem("x_sum_ready"), sem("x_top_ready"), sem("x_link")
        x_scale, x_turned, x_hi_ready, x_t_ready = (sem(n) for n in ("x_scale", "x_turned", "x_hi_ready", "x_t_ready"))
        proj_mm, proj_ready = sem("proj_mm"), sem("proj_ready")
        out_turned, rows_ready, out_ready = sem("out_turned"), sem("rows_ready"), sem("out_ready")
        r_mm, z_mm, c_mm = pair("r_mm"), sem("z_mm"), pair("c_mm")
        r_part, r_pre, r_gate = pair("r_part"), pair("r_pre"), pair("r_gate")
        rh_hi, rh_full, rh_lo = pair("rh_hi"), pair("rh_full"), pair("rh_lo")
        z_part, z_pre, z_keep = sem("z_part"), sem("z_pre"), sem("z_keep")
        c_part, c_pre, c_gate = pair("c_part"), pair("c_pre"), pair("c_gate")
        h_terms, h_hi, h_full, h_lo = pair("h_terms"), pair("h_hi"), pair("h_full"), pair("h_lo")

        block = ctx.enter_context(nc.Block())

        @block.sync
        def _(sp):
            def load_x(n, j, buffers, done):
                for t in range(TU):
                    sp.dma_start(buffers[j][t * B:(t + 1) * B], x_rows[n, t]).then_inc(done[j], 16)

            sp.dma_start(cond_nat[:], cond).then_inc(s_small_in, 16)
            for g, b in enumerate((b_r, b_z, b_h)):
                sp.dma_start(bias_nat[g * M:(g + 1) * M], b.rearrange("(m p) -> m p", p=P)).then_inc(s_small_in, 16)
            for j in range(BODY):
                load_x(j, j, x_nat, x_in)
            for g, c in enumerate((C_r, C_z, C_h)):
                sp.dma_start(c_stage[:, g], c.rearrange("(k p) e -> p k e", p=P)).then_inc(s_c_in[g], 16)
            for g, (w, u) in enumerate(((W_r, U_r), (W_z, U_z), (W_h, U_h))):
                sp.dma_start(w_stage[:, g], w.rearrange("(k p) e -> p k e", p=P)).then_inc(s_w_in[g], 16)
                sp.dma_start(u_stage[:, g], u.rearrange("(k p) e -> p k e", p=P)).then_inc(s_u_in[g], 16)
            for j in range(BODY):
                load_x(j, j, result, result_in)

            def block_of_steps(i, j, last):
                n = i * BODY + j
                tiles = NU * n + NU + 2 if last else sp.snap(NU * n + NU + 2)
                sp.wait_ge(out_ready, tiles)
                for t in range(TU):
                    sp.dma_start(out_rows[n, t], result[j][t * B:(t + 1) * B]).then_inc(result_out[j], 16)
                sp.wait_ge(result_out[j], (i + 1) * 16 * TU)
                if not last:
                    load_x(n + BODY, j, result, result_in)

            with sp.Fori(0, PASSES - 1) as i:
                for j in range(BODY):
                    block_of_steps(i, j, False)
            for j in range(BODY):
                block_of_steps(PASSES - 1, j, True)

        @block.gpsimd
        def _(pool):
            nc.gpsimd.memset(ident[:], 0.0).then_inc(s_zeroed, 1)
            nc.gpsimd.memset(state[:], 0.0).then_inc(s_const, 1)
            nc.gpsimd.memset(state_parts[:], 0.0).then_inc(s_const, 1)
            pool.wait_ge(s_const, 2)
            for j in range(2):
                pool.sem_inc(h_hi[j], 1)
                pool.sem_inc(h_lo[j], 1)
            pool.wait_ge(s_zeroed, 1)
            nc.gpsimd.affine_select(out=ident[:], in_=ident[:], compare_op=ALU.not_equal, fill=1.0, base=0,
                                    pattern=[[-1, P]], channel_multiplier=1).then_inc(s_const, 1)

            def top_of_x(n, j):
                nc.gpsimd.partition_all_reduce(x_top[j][:], x_sum[j][:], P, bass.bass_isa.ReduceOp.max)\
                    .then_inc(x_top_ready, 1)

            def x_rest(n, u):
                nc.gpsimd.tensor_tensor(x_lo[n][:, :, u, :], x_whole[u][:], x_hi[n][:, :, u, :], ALU.subtract)\
                    .then_inc(x_t_ready, 1)

            for n in range(BODY):
                pool.wait_ge(x_sum_ready, NU * n + NU)
                top_of_x(n, n)
            for n in range(BODY):
                for u in range(NU):
                    pool.wait_ge(x_hi_ready, NU * n + u + 1)
                    x_rest(n, u)
            for g in range(G):
                for part, ready, top, done in ((w_sum, s_w_sum, w_top, s_w_top), (u_sum, s_u_sum, u_top, s_u_top)):
                    pool.wait_ge(ready, g + 1)
                    nc.gpsimd.partition_all_reduce(top[g][:], part[g][:], P, bass.bass_isa.ReduceOp.max)\
                        .then_inc(done, 1)

            def add_rows(j, u, count):
                pool.wait_ge(rows_ready, count)
                nc.gpsimd.tensor_tensor(result[j][:, u], result[j][:, u], h_rows[:], ALU.add).then_inc(out_ready, 1)

            pool.wait_ge(result_in[1], 16 * TU)

            def block_of_steps(i, j, last):
                n = i * BODY + j
                for t in range(TB):
                    now = n * TB + t + 1 if last else pool.snap(n * TB + t + 1)
                    twice = 2 * (n * TB + t + 1) if last else pool.snap(2 * (n * TB + t + 1))
                    old = state[:, :, (t - 1) % TB, :]
                    pool.wait_ge(r_gate[0], now)
                    nc.gpsimd.tensor_tensor(reset_full[:, 0:HM], gate[:, R, 0:HM], old[:, 0:HM], ALU.mult)\
                        .then_inc(rh_full[0], 1)
                    if not last and t == X_TOP:
                        pool.wait_ge(x_sum_ready, NU * n + NU * BODY + NU)
                    pool.wait_ge(rh_full[0], now)
                    pool.wait_ge(rh_hi[0], now)
                    nc.gpsimd.tensor_tensor(reset_parts[:, 0:HM, B:2 * B], reset_full[:, 0:HM],
                                            reset_parts[:, 0:HM, 0:B], ALU.subtract).then_inc(rh_lo[0], 1)
                    if not last and t == X_TOP:
                        top_of_x(n + BODY, j)
                    pool.wait_ge(z_keep, now)
                    nc.gpsimd.tensor_tensor(kept[:], keep[:], old, ALU.mult).then_inc(h_terms[0], 1)
                    for half in range(2):
                        hm = halves(half)
                        pool.wait_ge(h_terms[half], (twice, now)[half])
                        nc.gpsimd.tensor_tensor(state[:, hm, t, :], taken[:, hm], kept[:, hm], ALU.add)\
                            .then_inc(h_full[half], 1)
                    if t in H_ROWS:
                        u = H_ROWS.index(t)
                        count = NU * n + u + 2 if last else pool.snap(NU * n + u + 2)
                        if u == 1:
                            pool.wait_ge(result_in[j], (i + 1) * 16 * TU)
                        add_rows(j if u else 1 - j, 1 - u, count)
                    if not last and t - 1 in X_TURN:
                        u = X_TURN.index(t - 1)
                        pool.wait_ge(x_hi_ready, NU * n + NU * BODY + u + 1)
                        x_rest(j, u)

            with pool.Fori(0, PASSES - 1) as i:
                for j in range(BODY):
                    block_of_steps(i, j, False)
            for j in range(BODY):
                block_of_steps(PASSES - 1, j, True)
            add_rows(BODY - 1, 1, BLOCKS * NU + 2)

        @block.tensor
        def _(pe):
            pe.wait_ge(s_const, 3)
            pe.wait_ge(s_small_in, 16 * (1 + G))
            for k in range(KD):
                nc.tensor.transpose(t_bank[:, k * B:(k + 1) * B], cond_nat[:, k * P:(k + 1) * P], ident[0:B, 0:B])
            nc.tensor.transpose(t_bank[:, KD * B:KD * B + GROUPS], bias_nat[:], ident[0:GROUPS, 0:GROUPS])\
                .then_inc(s_small_turned, 1)

            def turn(tiles):
                for k, tile in enumerate(tiles):
                    last = nc.tensor.transpose(t_bank[:, k * P:(k + 1) * P], tile, ident[:])
                return last

            def turn_x(j, u):
                turn([x_nat[j][:, u, k * P:(k + 1) * P] for k in range(KD)]).then_inc(x_turned, 1)

            def turn_state(u):
                turn([state[:, m, u * TU:(u + 1) * TU, :] for m in range(M)]).then_inc(out_turned, 1)

            def project(first, j, f0, f1):
                for f in range(f0, f1):
                    q, c = divmod(f, PRODUCTS)
                    k, c = divmod(c, PARTS)
                    g, m = divmod(q, M)
                    if k == 0 and c == 0 and not (q < 2 and isinstance(first, int) and first == 0):
                        pe.wait_ge(proj_ready, first + (q - 1))
                    w, xs = ((w_hi, x_hi), (w_hi, x_lo), (w_lo, x_hi))[c]
                    last = nc.tensor.matmul(p_bank[q % 2][:, 0:COLS], w[:, g, k, m * P:(m + 1) * P],
                                            xs[j][:, k, :, :], start=(k == 0 and c == 0),
                                            stop=(k == KD - 1 and c == PARTS - 1))
                    if k == KD - 1 and c == PARTS - 1:
                        last.then_inc(proj_mm, 1)

            def times_u_lo(g, banks, parts, hi_ready, now, which=(0, 1)):
                per = M // len(banks)
                for half in which:
                    pe.wait_ge(hi_ready[half], now)
                    for m in range(M):
                        for k in range(half * HM, (half + 1) * HM):
                            nc.tensor.matmul(sums(banks[m // per], per)[:, m % per, 0:B],
                                             u_lo[:, g, k, m * P:(m + 1) * P], parts[:, k, 0:B],
                                             start=(half == 0 and k == 0 and m % per == 0), stop=False,
                                             skip_group_check=True)

            def times_u_hi(g, banks, parts, lo_ready, now, done, order):
                per = M // len(banks)
                for c, (half, b) in enumerate(order):
                    if half not in [h for h, _ in order[:c]]:
                        pe.wait_ge(lo_ready[half], now)
                    for m in range(per):
                        for k in range(half * HM, (half + 1) * HM):
                            last = nc.tensor.matmul(sums(banks[b], per)[:, m, :],
                                                    u_hi[:, g, k, (b * per + m) * P:(b * per + m + 1) * P],
                                                    parts[:, k, :],
                                                    start=False, stop=(k == KD - 1), skip_group_check=True)
                    if half == 1:
                        last.then_inc(done[b], 1)

            def first_x(n, u):
                if n + u == 0:
                    pe.wait_ge(s_small_ready, 1)
                else:
                    pe.wait_ge(x_hi_ready, NU * n + u)
                if u == 0:
                    pe.wait_ge(x_in[n], 16 * TU)
                turn_x(n, u)

            for n in range(BODY):
                for u in range(NU):
                    first_x(n, u)
            def cond_c(g, m0=0, m1=M):
                if m0 == 0:
                    pe.wait_ge(s_c_in[g], 16)
                for m in range(m0, m1):
                    for k in range(KD):
                        last = nc.tensor.matmul(base_bank[g][:, m * B:(m + 1) * B], c_stage[:, g, k, m * P:(m + 1) * P],
                                                cond_t[:, k, :], start=(k == 0), stop=(k == KD - 1))
                if m1 == M:
                    last.then_inc(s_base_mm, 1)

            def first_projection(g, m0=0, m1=M):
                if m0 == 0:
                    pe.wait_ge(s_w_split, g + 1)
                project(0, 0, (g * M + m0) * PRODUCTS, (g * M + m1) * PRODUCTS)

            cond_c(R)
            cond_c(Z, 0, HM)
            pe.wait_ge(x_t_ready, NU)
            first_projection(R, 0, HM)
            cond_c(Z, HM, M)
            first_projection(R, HM, M)
            cond_c(C)
            first_projection(Z)
            first_projection(C)
            pe.wait_ge(s_u_split, G)

            def block_of_steps(i, j, last):
                n = i * BODY + j
                fill = not (last and j == BODY - 1)
                first = n * GROUPS + GROUPS if last else pe.snap(n * GROUPS + GROUPS)
                for t in range(TB):
                    now = n * TB + t + 1 if last else pe.snap(n * TB + t + 1)
                    times_u_lo(R, r_bank, state_parts, h_hi, now, [0])
                    times_u_lo(Z, [z_bank], state_parts, h_hi, now, [0])
                    times_u_lo(R, r_bank, state_parts, h_hi, now, [1])
                    times_u_lo(Z, [z_bank], state_parts, h_hi, now, [1])
                    times_u_hi(R, r_bank, state_parts, h_lo, now, r_mm, R_ORDER)
                    times_u_hi(Z, [z_bank], state_parts, h_lo, now, [z_mm], ((0, 0), (1, 0)))
                    if t == H_TURN[0]:
                        pe.wait_ge(x_hi_ready, BLOCKS * NU if last else NU * n + NU * BODY)
                        pe.wait_ge(rows_ready, NU * n + 1)
                        turn_state(1)
                    if t == H_TURN[1]:
                        if last:
                            pe.wait_ge(rows_ready, NU * n + 2)
                        pe.wait_ge(x_hi_ready, BLOCKS * NU if last else NU * n + NU * BODY + NU)
                        turn_state(0)
                    if fill:
                        if t == 0:
                            pe.wait_ge(x_t_ready, NU * n + 2 * NU)
                        project(first, 1 - j, START[t], START[t] + BEFORE_C[t])
                    times_u_lo(C, c_bank, reset_parts, rh_hi, now)
                    if fill:
                        project(first, 1 - j, START[t] + BEFORE_C[t], START[t] + BEFORE_C[t] + 1)
                    times_u_hi(C, c_bank, reset_parts, rh_lo, now, c_mm, C_ORDER)
                    if not last and t in X_TURN:
                        u = X_TURN.index(t)
                        if u == 0:
                            pe.wait_ge(rows_ready, NU * n + 2)
                            pe.wait_ge(x_in[j], (i + 2) * 16 * TU)
                        else:
                            pe.wait_ge(x_hi_ready, NU * n + NU * BODY + u)
                        turn_x(j, u)
                    if fill:
                        project(first, 1 - j, START[t] + BEFORE_C[t] + 1, START[t + 1])

            with pe.Fori(0, PASSES - 1) as i:
                for j in range(BODY):
                    block_of_steps(i, j, False)
            for j in range(BODY):
                block_of_steps(PASSES - 1, j, True)
            for half in range(2):
                pe.wait_ge(h_full[half], T)
            pe.wait_ge(rows_ready, BLOCKS * NU + 1)
            turn_state(1)

        @block.scalar
        def _(act):
            def sum_x(j, u):
                nc.scalar.activation(x_abs[:], x_nat[j][:, u], ACT.Abs, accum_out=x_sum[j][:, u:u + 1])\
                    .then_inc(x_sum_ready, 1)

            def copy_x(n, j, u):
                act.wait_ge(x_turned, NU * n + u + 1)
                tile = t_bank[:, 0:KD * P].rearrange("p (k c) -> p k c", k=KD)
                nc.scalar.activation(x_whole[u][:], tile, ACT.Copy, scale=x_up[j][:])
                nc.scalar.activation(x_hi[j][:, :, u, :], tile, ACT.Copy, scale=x_up[j][:]).then_inc(x_hi_ready, 1)

            def copy_rows(v):
                act.wait_ge(out_turned, v)
                act.wait_ge(out_ready, v)
                nc.scalar.activation(h_rows[:], t_bank[:, 0:E], ACT.Copy, scale=1.0 / HSCALE).then_inc(rows_ready, 1)

            def load_x(n, j):
                for t in range(TU):
                    act.dma_start(x_nat[j][t * B:(t + 1) * B], x_rows[n, t]).then_inc(x_in[j], 16)

            for n in range(BODY):
                act.wait_ge(x_in[n], 16 * TU)
                for u in range(NU):
                    if n + u:
                        act.wait_ge(x_sum_ready, NU * n + u)
                    sum_x(n, u)
            for n in range(BODY):
                act.wait_ge(x_scale, n + 1)
                for u in range(NU):
                    if n > 0:
                        act.wait_ge(x_t_ready, NU * (n - 1) + u + 1)
                    copy_x(n, n, u)
                load_x(n + BODY, n)
            def hi_of(stage, hi, g, up, ready, done):
                act.wait_ge(ready, g + 1)
                nc.scalar.activation(hi[:, g], stage[:, g], ACT.Copy, scale=up[:, g:g + 1]).then_inc(done, 1)

            def sum_of(stage, hi, g, loaded, total, done):
                act.wait_ge(loaded[g], 16)
                nc.scalar.activation(hi[:, g].bitcast(bf16), stage[:, g], ACT.Abs, accum_out=total[g][:])\
                    .then_inc(done, 1)

            for g in range(G):
                sum_of(w_stage, w_hi, g, s_w_in, w_sum, s_w_sum)
                hi_of(w_stage, w_hi, g, w_up, s_w_scale, s_w_hi)
                sum_of(u_stage, u_hi, g, s_u_in, u_sum, s_u_sum)
                hi_of(u_stage, u_hi, g, u_up, s_u_scale, s_u_hi)
            act.wait_ge(s_units, G)
            scales = []
            for name, scale in (("r", down[0:1, R:R + 1]), ("z", down[0:1, Z:Z + 1]), ("c", down[0:1, C:C + 1]),
                                ("keep", down_neg[0:1, Z:Z + 1])):
                scales.append(act.alloc_register(f"scale_{name}"))
                act.reg_load(scales[-1], scale.bitcast(i32))
            scale_r, scale_z, scale_c, scale_keep = scales

            def block_of_steps(i, j, last):
                n = i * BODY + j
                for t in range(TB):
                    now = n * TB + t + 1 if last else act.snap(n * TB + t + 1)
                    for half in range(2):
                        act.wait_ge(r_pre[half], now)
                        nc.scalar.activation(gate[:, R, halves(half)], pre_b[:, R, halves(half)], ACT.Sigmoid,
                                             scale=scale_r).then_inc(r_gate[half], 1)
                    act.wait_ge(z_pre, now)
                    nc.scalar.activation(keep[:], pre_b[:, Z], ACT.Sigmoid, scale=scale_keep)\
                        .then_inc(z_keep, 1)
                    nc.scalar.activation(gate[:, Z], pre_b[:, Z], ACT.Sigmoid, scale=scale_z)
                    for half in range(2):
                        act.wait_ge(c_pre[half], now)
                        nc.scalar.activation(gate[:, C, halves(half)], pre_b[:, C, halves(half)], ACT.Tanh,
                                             scale=scale_c).then_inc(c_gate[half], 1)
                    if t in H_ROWS:
                        v = NU * n + H_ROWS.index(t) + 1
                        copy_rows(v if last else act.snap(v))
                    if not last and t == X_SUM:
                        act.wait_ge(x_in[j], (i + 2) * 16 * TU)
                        for u in range(NU):
                            act.wait_ge(x_sum_ready, NU * (n + BODY) + u)
                            sum_x(j, u)
                    if not last and t in X_TURN:
                        u = X_TURN.index(t)
                        if u == 0:
                            act.wait_ge(x_scale, n + BODY + 1)
                        act.wait_ge(x_t_ready, NU * (n + BODY - 1) + u + 1)
                        copy_x(n + BODY, j, u)
                    if not last and t == X_LOAD:
                        load_x((n + 2 * BODY) % BLOCKS, j)

            with act.Fori(0, PASSES - 1) as i:
                for j in range(BODY):
                    block_of_steps(i, j, False)
            for j in range(BODY):
                block_of_steps(PASSES - 1, j, True)
            copy_rows(BLOCKS * NU + 1)
            for j in range(BODY):
                act.wait_ge(x_in[j], (PASSES + 1) * 16 * TU)

        @block.vector
        def _(dve):
            V = nc.vector
            links = [0]

            def link(ins):
                links[0] += 1
                ins.then_inc(s_link, 1)
                dve.wait_ge(s_link, links[0])

            dve.wait_ge(s_small_turned, 1)
            V.tensor_copy(bias_t[:], t_bank[:, KD * B:KD * B + GROUPS]).then_inc(s_link, 1)
            V.tensor_copy(cond_t[:], t_bank[:, 0:KD * B].rearrange("p (k b) -> p k b", k=KD)).then_inc(s_link, 1)
            links[0] = 2
            dve.wait_ge(s_link, 2)
            dve.sem_inc(s_small_ready, 1)
            dve.sem_inc(rows_ready, 1)
            dve.sem_inc(out_ready, 1)

            def power_of(out_, in_):
                link(V.tensor_scalar(out_.bitcast(i32), in_.bitcast(i32), 0x7F800000, None, ALU.bitwise_and))
                link(V.tensor_scalar(out_, out_, LEAST, None, ALU.max))

            def scale_of(out_, power_, pow_):
                return V.tensor_scalar(out_.bitcast(i32), power_.bitcast(i32), -1.0, float((254 + pow_) << 23),
                                       ALU.mult, ALU.add)

            def split(stage, hi, lo, g, scale, ready, done):
                dve.wait_ge(ready, g + 1)
                V.scalar_tensor_tensor(lo[:, g].rearrange("p k e -> p (k e)"), stage[:, g].rearrange("p k e -> p (k e)"),
                                       scale[:, g:g + 1], hi[:, g].rearrange("p k e -> p (k e)"),
                                       ALU.mult, ALU.subtract).then_inc(done, 1)

            def x_scale_step(n, j, c, first=False):
                if c:
                    dve.wait_ge(x_link, 3 * n + c)
                if c == 0:
                    dve.wait_ge(x_top_ready, n + 1)
                    V.tensor_reduce(x_pow[j][:], x_top[j][:], AX.X, ALU.max).then_inc(x_link, 1)
                elif c == 1:
                    V.tensor_scalar(x_pow[j][:].bitcast(i32), x_pow[j][:].bitcast(i32), 0x7F800000, None,
                                    ALU.bitwise_and).then_inc(x_link, 1)
                elif c == 2:
                    V.tensor_scalar(x_pow[j][:], x_pow[j][:], LEAST, None, ALU.max).then_inc(x_link, 1)
                else:
                    if not first:
                        V.tensor_scalar(x_down[j][:], w_down[:], x_pow[j][:], None, ALU.mult)
                    scale_of(x_up[j][:], x_pow[j][:], POW).then_inc(x_scale, 1)

            def take_projection(first, j, q):
                dve.wait_ge(proj_mm, first + q + 1)
                V.scalar_tensor_tensor(proj[j][:, q], p_bank[q % 2][:, 0:COLS].rearrange("p (t b) -> p t b", t=TB),
                                       x_down[j][:, q // M:q // M + 1],
                                       base[:, q, :].unsqueeze(1).to_broadcast([P, TB, B]),
                                       ALU.mult, ALU.add).then_inc(proj_ready, 1)

            def scale_w(g):
                w = slice(g, g + 1)
                dve.wait_ge(s_w_top, g + 1)
                power_of(w_pow[:, w], w_top[g][:])
                scale_of(w_up[:, w], w_pow[:, w], POW).then_inc(s_w_scale, 1)

            def scale_u(g):
                w, r = slice(g, g + 1), slice(g * M, (g + 1) * M)
                dve.wait_ge(s_u_top, g + 1)
                power_of(u_pow[:, w], u_top[g][:])
                scale_of(u_up[:, w], u_pow[:, w], POW).then_inc(s_u_scale, 1)
                dve.wait_ge(s_base_mm, g + 1)
                V.tensor_tensor(base[:, r], base_bank[g][:, 0:M * B].rearrange("p (q b) -> p q b", q=M),
                                bias_t[:, r].unsqueeze(2).to_broadcast([P, M, B]), ALU.add)
                dve.wait_ge(s_u_scale, g + 1)
                V.tensor_scalar(down[:, w], u_pow[:, w], 2.0 ** -POW / HSCALE, None, ALU.mult)
                link(V.tensor_scalar(units[:, w], u_up[:, w], HSCALE, None, ALU.mult))
                V.tensor_scalar(down_neg[:, w], down[:, w], -1.0, None, ALU.mult).then_inc(s_units, 1)
                V.tensor_scalar(base[:, r], base[:, r], units[:, w], None, ALU.mult)
                link(V.scalar_tensor_tensor(w_down[:, w], w_pow[:, w], 2.0 ** (-2 * POW), units[:, w],
                                            ALU.mult, ALU.mult))
                for n in range(BODY):
                    ins = V.tensor_scalar(x_down[n][:, w], x_pow[n][:], w_down[:, w], None, ALU.mult)
                link(ins)

            def take_first(g, part):
                for q in range(g * M + part * HM, g * M + (part + 1) * HM):
                    take_projection(0, 0, q)

            def split_u(g):
                split(u_stage, u_hi, u_lo, g, u_up, s_u_hi, s_u_split)

            for n in range(BODY):
                for c in range(4):
                    x_scale_step(n, n, c, first=True)
            for g in range(G):
                scale_w(g)
                if g > 0:
                    take_first(g - 1, 1)
                split(w_stage, w_hi, w_lo, g, w_up, s_w_hi, s_w_split)
                if g == C:
                    split_u(Z)
                scale_u(g)
                if g == R:
                    split_u(R)
                take_first(g, 0)
            split_u(C)
            take_first(C, 1)
            dve.wait_ge(proj_ready, GROUPS)

            def add_hi(g, j, t, m0, m1, b, part):
                V.tensor_tensor(pre_a[:, g, m0:m1], sums(b, m1 - m0)[:, :, 0:B],
                                proj[j][:, g * M + m0:g * M + m1, t, :], ALU.add).then_inc(part, 1)

            def add_lo(g, m0, m1, b, part, pre, now):
                dve.wait_ge(part, now)
                V.tensor_tensor(pre_b[:, g, m0:m1], sums(b, m1 - m0)[:, :, B:2 * B], pre_a[:, g, m0:m1],
                                ALU.add).then_inc(pre, 1)

            def block_of_steps(i, j, last):
                n = i * BODY + j
                fill = not (last and j == BODY - 1)
                first = n * GROUPS + GROUPS if last else dve.snap(n * GROUPS + GROUPS)

                def between(t, late, x_steps):
                    for c in x_steps[t][:1] if not last and t in x_steps else ():
                        x_scale_step(n + BODY, j, c)
                    for q in takes[2 * t + late] if fill else ():
                        take_projection(first, 1 - j, q)
                    for c in x_steps[t][1:] if not last and t in x_steps else ():
                        x_scale_step(n + BODY, j, c)

                for t in range(TB):
                    now = n * TB + t + 1 if last else dve.snap(n * TB + t + 1)
                    twice = 2 * (n * TB + t + 1) if last else dve.snap(2 * (n * TB + t + 1))
                    old = state[:, :, (t - 1) % TB, :]
                    new = state[:, :, t, :]
                    for half in range(2):
                        dve.wait_ge(r_mm[half], now)
                        add_hi(R, j, t, half * HM, (half + 1) * HM, r_bank[half], r_part[half])
                    for half in range(2):
                        add_lo(R, half * HM, (half + 1) * HM, r_bank[half], r_part[half], r_pre[half], now)
                    dve.wait_ge(z_mm, now)
                    add_hi(Z, j, t, 0, M, z_bank, z_part)
                    for half in range(2):
                        hm = halves(half)
                        dve.wait_ge(r_gate[half], now)
                        V.tensor_tensor(reset_parts[:, hm, 0:B], gate[:, R, hm], old[:, hm], ALU.mult)\
                            .then_inc(rh_hi[half], 1)
                    V.tensor_tensor(reset_full[:, hm], gate[:, R, hm], old[:, hm], ALU.mult).then_inc(rh_full[1], 1)
                    if t == 0:
                        dve.wait_ge(proj_ready, first)
                    add_lo(Z, 0, M, z_bank, z_part, z_pre, now)
                    dve.wait_ge(rh_full[1], now)
                    V.tensor_tensor(reset_parts[:, hm, B:2 * B], reset_full[:, hm],
                                    reset_parts[:, hm, 0:B], ALU.subtract).then_inc(rh_lo[1], 1)
                    if t == TB - 1 and fill:
                        dve.wait_ge(proj_ready, first + C * M)
                    between(t, 0, X_SCALE_EARLY)
                    for half in range(2):
                        dve.wait_ge(c_mm[half], now)
                        add_hi(C, j, t, half * HM, (half + 1) * HM, c_bank[half], c_part[half])
                        add_lo(C, half * HM, (half + 1) * HM, c_bank[half], c_part[half], c_pre[half], now)
                    for half in range(2):
                        hm = halves(half)
                        dve.wait_ge(c_gate[half], now)
                        V.scalar_tensor_tensor(taken[:, hm], gate[:, C, hm], HSCALE, gate[:, Z, hm],
                                               ALU.mult, ALU.mult).then_inc(h_terms[half], 1)
                        dve.wait_ge(h_terms[half], (twice, now)[half])
                        V.tensor_tensor(state_parts[:, hm, 0:B], taken[:, hm], kept[:, hm], ALU.add)\
                            .then_inc(h_hi[half], 1)
                    for half in range(2):
                        hm = halves(half)
                        dve.wait_ge(h_hi[half], now + 1)
                        dve.wait_ge(h_full[half], now)
                        V.tensor_tensor(state_parts[:, hm, B:2 * B], new[:, hm], state_parts[:, hm, 0:B],
                                        ALU.subtract).then_inc(h_lo[half], 1)
                    between(t, 1, X_SCALE_LATE)

            with dve.Fori(0, PASSES - 1) as i:
                for j in range(BODY):
                    block_of_steps(i, j, False)
            for j in range(BODY):
                block_of_steps(PASSES - 1, j, True)


_INS = ["x", "cond_1024", "L0_cond_W_z", "L0_cond_U_z", "L0_cond_C_z", "L0_cond_b_z", "L0_cond_W_r", "L0_cond_U_r",
        "L0_cond_C_r", "L0_cond_b_r", "L0_cond_W", "L0_cond_U", "L0_cond_C", "L0_cond_b"]


def kernel(**inputs):
    import numpy as _np
    import concourse.bacc as _bacc
    from concourse import mybir as _mybir
    from concourse.bass_utils import run_bass_kernel_spmd as _run

    nc = _bacc.Bacc("TRN2", target_bir_lowering=False, num_devices=1)
    arrays, args = {}, []
    for name in _INS:
        a = _np.ascontiguousarray(inputs[name])
        arrays[f"in_{name}_dram"] = a
        args.append(nc.dram_tensor(f"in_{name}_dram", a.shape, _mybir.dt.from_np(a.dtype), kind="ExternalInput").ap())
    shape = inputs["x"].shape
    args.append(nc.dram_tensor("out_dram", shape, _mybir.dt.float32, kind="ExternalOutput").ap())
    conditioned_gru_residual_kernel(nc, *args)
    r = _run(nc, [arrays], core_ids=[0])
    return r.results[0]["out_dram"]
```
